# Optimizing a Trainium2 kernel written in Bass

```python
import numpy as np
import jax
import jax.numpy as jnp

def _softmax(x, axis=-1):
    return jax.nn.softmax(x, axis=axis)

def _gelu(x):
    return jax.nn.gelu(x, approximate=True)

def _silu(x):
    return jax.nn.silu(x)

def _sigmoid(x):
    return jax.nn.sigmoid(x)

def _layernorm(x, axis=-1, eps=1e-05):
    m = jnp.mean(x, axis=axis, keepdims=True)
    v = jnp.var(x, axis=axis, keepdims=True)
    return (x - m) / jnp.sqrt(v + eps)

def _scatter_add(tgt, idx, src, axis=0):
    return tgt.at[idx].add(src)

def _segment_sum(src, seg, n):
    return jax.ops.segment_sum(src, seg, n)
kernel_name = 'mk_dlrm_tower_d1_rec_r8_1731fd'

def setup_inputs(seed: int=0):
    np.random.seed(seed)
    _w = jnp.asarray

    def _rec_inputs():
        import jax
        import jax.numpy as jnp
        _tk = jax.random.key(seed)
        ids = jnp.stack([jax.random.randint(jax.random.fold_in(_tk, 200 + f), (2048,), 0, v, jnp.int32) for f, v in enumerate([1000, 1250, 125000, 1250, 1250, 12500, 1000, 1250, 1250, 1250, 1250, 1000, 1250, 1000, 1000, 1000, 1000, 1250, 12500, 12500, 1000, 12500, 12500, 1250, 1000, 1000])], axis=1)
        tbl_0 = 0.05 * jax.random.normal(jax.random.fold_in(_tk, 500 + 0), (1000, 128), jnp.float32)
        tbl_1 = 0.05 * jax.random.normal(jax.random.fold_in(_tk, 500 + 1), (1250, 128), jnp.float32)
        tbl_2 = 0.05 * jax.random.normal(jax.random.fold_in(_tk, 500 + 2), (125000, 128), jnp.float32)
        tbl_3 = 0.05 * jax.random.normal(jax.random.fold_in(_tk, 500 + 3), (1250, 128), jnp.float32)
        tbl_4 = 0.05 * jax.random.normal(jax.random.fold_in(_tk, 500 + 4), (1250, 128), jnp.float32)
        tbl_5 = 0.05 * jax.random.normal(jax.random.fold_in(_tk, 500 + 5), (12500, 128), jnp.float32)
        tbl_6 = 0.05 * jax.random.normal(jax.random.fold_in(_tk, 500 + 6), (1000, 128), jnp.float32)
        tbl_7 = 0.05 * jax.random.normal(jax.random.fold_in(_tk, 500 + 7), (1250, 128), jnp.float32)
        tbl_8 = 0.05 * jax.random.normal(jax.random.fold_in(_tk, 500 + 8), (1250, 128), jnp.float32)
        tbl_9 = 0.05 * jax.random.normal(jax.random.fold_in(_tk, 500 + 9), (1250, 128), jnp.float32)
        tbl_10 = 0.05 * jax.random.normal(jax.random.fold_in(_tk, 500 + 10), (1250, 128), jnp.float32)
        tbl_11 = 0.05 * jax.random.normal(jax.random.fold_in(_tk, 500 + 11), (1000, 128), jnp.float32)
        tbl_12 = 0.05 * jax.random.normal(jax.random.fold_in(_tk, 500 + 12), (1250, 128), jnp.float32)
        tbl_13 = 0.05 * jax.random.normal(jax.random.fold_in(_tk, 500 + 13), (1000, 128), jnp.float32)
        tbl_14 = 0.05 * jax.random.normal(jax.random.fold_in(_tk, 500 + 14), (1000, 128), jnp.float32)
        tbl_15 = 0.05 * jax.random.normal(jax.random.fold_in(_tk, 500 + 15), (1000, 128), jnp.float32)
        tbl_16 = 0.05 * jax.random.normal(jax.random.fold_in(_tk, 500 + 16), (1000, 128), jnp.float32)
        tbl_17 = 0.05 * jax.random.normal(jax.random.fold_in(_tk, 500 + 17), (1250, 128), jnp.float32)
        tbl_18 = 0.05 * jax.random.normal(jax.random.fold_in(_tk, 500 + 18), (12500, 128), jnp.float32)
        tbl_19 = 0.05 * jax.random.normal(jax.random.fold_in(_tk, 500 + 19), (12500, 128), jnp.float32)
        tbl_20 = 0.05 * jax.random.normal(jax.random.fold_in(_tk, 500 + 20), (1000, 128), jnp.float32)
        tbl_21 = 0.05 * jax.random.normal(jax.random.fold_in(_tk, 500 + 21), (12500, 128), jnp.float32)
        tbl_22 = 0.05 * jax.random.normal(jax.random.fold_in(_tk, 500 + 22), (12500, 128), jnp.float32)
        tbl_23 = 0.05 * jax.random.normal(jax.random.fold_in(_tk, 500 + 23), (1250, 128), jnp.float32)
        tbl_24 = 0.05 * jax.random.normal(jax.random.fold_in(_tk, 500 + 24), (1000, 128), jnp.float32)
        tbl_25 = 0.05 * jax.random.normal(jax.random.fold_in(_tk, 500 + 25), (1000, 128), jnp.float32)
        _rk = jax.random.fold_in(_tk, 7)
        r_dense_x = -0.000514642 + 1.00011 * jax.random.normal(jax.random.fold_in(_rk, 101), (2048, 128), jnp.float32)
        W_top1 = 0.0456912 * jax.random.normal(jax.random.fold_in(_tk, 801), (479, 512), jnp.float32)
        W_top2 = 0.0441942 * jax.random.normal(jax.random.fold_in(_tk, 802), (512, 256), jnp.float32)
        W_top3 = 0.0625 * jax.random.normal(jax.random.fold_in(_tk, 803), (256, 1), jnp.float32)
        b_top1 = jnp.zeros((512,), jnp.float32)
        b_top2 = jnp.zeros((256,), jnp.float32)
        return (r_dense_x, ids, tbl_0, tbl_1, tbl_2, tbl_3, tbl_4, tbl_5, tbl_6, tbl_7, tbl_8, tbl_9, tbl_10, tbl_11, tbl_12, tbl_13, tbl_14, tbl_15, tbl_16, tbl_17, tbl_18, tbl_19, tbl_20, tbl_21, tbl_22, tbl_23, tbl_24, tbl_25, W_top1, b_top1, W_top2, b_top2, W_top3)
    r_dense_x, ids, tbl_0, tbl_1, tbl_2, tbl_3, tbl_4, tbl_5, tbl_6, tbl_7, tbl_8, tbl_9, tbl_10, tbl_11, tbl_12, tbl_13, tbl_14, tbl_15, tbl_16, tbl_17, tbl_18, tbl_19, tbl_20, tbl_21, tbl_22, tbl_23, tbl_24, tbl_25, W_top1, b_top1, W_top2, b_top2, W_top3 = _rec_inputs()

    def _L0_rec_setup():
        import jax, jax.numpy as jnp
        import numpy as np
        F = 26
        D = 128
        B = 2048
        _TRIU_I, _TRIU_J = np.triu_indices(F + 1, k=1)
        _TRIU_I = jnp.asarray(_TRIU_I)
        _TRIU_J = jnp.asarray(_TRIU_J)
        key = jax.random.key(seed)
        k1, k2 = jax.random.split(key)
        sparse_x = jax.random.normal(k1, (B, F, D), dtype=jnp.float32)
        dense_x = jax.random.normal(k2, (B, D), dtype=jnp.float32)
        return {'sparse_x': sparse_x, 'dense_x': dense_x}
    _L0_rec_all = _L0_rec_setup()
    _L0_rec_in = {k: v for k, v in _L0_rec_all.items() if k in ()}
    del _L0_rec_all
    return {'r_dense_x': r_dense_x, 'ids': ids, 'tbl_0': tbl_0, 'tbl_1': tbl_1, 'tbl_2': tbl_2, 'tbl_3': tbl_3, 'tbl_4': tbl_4, 'tbl_5': tbl_5, 'tbl_6': tbl_6, 'tbl_7': tbl_7, 'tbl_8': tbl_8, 'tbl_9': tbl_9, 'tbl_10': tbl_10, 'tbl_11': tbl_11, 'tbl_12': tbl_12, 'tbl_13': tbl_13, 'tbl_14': tbl_14, 'tbl_15': tbl_15, 'tbl_16': tbl_16, 'tbl_17': tbl_17, 'tbl_18': tbl_18, 'tbl_19': tbl_19, 'tbl_20': tbl_20, 'tbl_21': tbl_21, 'tbl_22': tbl_22, 'tbl_23': tbl_23, 'tbl_24': tbl_24, 'tbl_25': tbl_25, 'W_top1': W_top1, 'b_top1': b_top1, 'W_top2': W_top2, 'b_top2': b_top2, 'W_top3': W_top3}

def reference(r_dense_x, ids, tbl_0, tbl_1, tbl_2, tbl_3, tbl_4, tbl_5, tbl_6, tbl_7, tbl_8, tbl_9, tbl_10, tbl_11, tbl_12, tbl_13, tbl_14, tbl_15, tbl_16, tbl_17, tbl_18, tbl_19, tbl_20, tbl_21, tbl_22, tbl_23, tbl_24, tbl_25, W_top1, b_top1, W_top2, b_top2, W_top3):
    import jax
    import jax.numpy as jnp

    def _L0_rec_ref(sparse_x, dense_x):
        import jax, jax.numpy as jnp
        import numpy as np
        F = 26
        D = 128
        B = 2048
        _TRIU_I, _TRIU_J = np.triu_indices(F + 1, k=1)
        _TRIU_I = jnp.asarray(_TRIU_I)
        _TRIU_J = jnp.asarray(_TRIU_J)
        combined = jnp.concatenate([sparse_x, dense_x[:, None, :]], axis=1)
        interact = jnp.einsum('bfd,bgd->bfg', combined, combined)
        return interact[:, _TRIU_I, _TRIU_J]
    e = jnp.stack([tbl_0[ids[:, 0]], tbl_1[ids[:, 1]], tbl_2[ids[:, 2]], tbl_3[ids[:, 3]], tbl_4[ids[:, 4]], tbl_5[ids[:, 5]], tbl_6[ids[:, 6]], tbl_7[ids[:, 7]], tbl_8[ids[:, 8]], tbl_9[ids[:, 9]], tbl_10[ids[:, 10]], tbl_11[ids[:, 11]], tbl_12[ids[:, 12]], tbl_13[ids[:, 13]], tbl_14[ids[:, 14]], tbl_15[ids[:, 15]], tbl_16[ids[:, 16]], tbl_17[ids[:, 17]], tbl_18[ids[:, 18]], tbl_19[ids[:, 19]], tbl_20[ids[:, 20]], tbl_21[ids[:, 21]], tbl_22[ids[:, 22]], tbl_23[ids[:, 23]], tbl_24[ids[:, 24]], tbl_25[ids[:, 25]]], axis=1)
    z = _L0_rec_ref(e, r_dense_x)
    z = z.reshape(z.shape[0], -1)
    h = jnp.concatenate([z, r_dense_x], axis=1)
    h = jnp.maximum(h @ W_top1 + b_top1, 0.0)
    h = jnp.maximum(h @ W_top2 + b_top2, 0.0)
    y = h @ W_top3
    return y

_drawn_inputs = setup_inputs


def setup_inputs(seed=0):
    import zlib

    import numpy as np

    out = dict(_drawn_inputs(seed))
    spreads = {'b_top1': (0.0, 0.1), 'b_top2': (0.0, 0.1)}
    factors = {}
    for name, (base, spread) in spreads.items():
        noise = np.random.default_rng([zlib.crc32(name.encode()), seed]).standard_normal(out[name].shape)
        drawn = base * np.exp(spread * noise) if base else spread * noise
        out[name] = jnp.asarray(drawn.astype(out[name].dtype))
    for name, factor in factors.items():
        out[name] = (out[name] * factor).astype(out[name].dtype)
    return out
```

```python
import numpy as np
import concourse.bass as bass
from concourse import mybir
from contextlib import ExitStack

TABLES = 26
FEATURES = TABLES + 1
D = 128
SAMPLES = 2048
H1, H2 = 512, 256
SMALL_PARTS = 125

BATCH = 256
BATCHES = SAMPLES // BATCH
TILE = 128
TILES = BATCH // TILE
QUADS = BATCH // 4
QUAD_ROWS = 32

TABLE_ROWS = [1000, 1250, 125000, 1250, 1250, 12500, 1000, 1250, 1250, 1250, 1250, 1000, 1250,
              1000, 1000, 1000, 1000, 1250, 12500, 12500, 1000, 12500, 12500, 1250, 1000, 1000]
ONEHOT_COUNT = 8
ONEHOT = sorted((f for f in range(TABLES) if TABLE_ROWS[f] <= 1250),
                key=lambda f: (TABLE_ROWS[f], f))[:ONEHOT_COUNT]
GATHERED = [f for f in range(TABLES) if f not in ONEHOT]
NOH, NG = len(ONEHOT), len(GATHERED)
FEATURE_AT = ONEHOT + GATHERED + [TABLES]
CHUNKS = [TABLE_ROWS[f] // SMALL_PARTS for f in ONEHOT]
CHUNK0 = [sum(CHUNKS[:n]) for n in range(NOH + 1)]
MAX_CHUNKS = max(CHUNKS)

SHIFTS = (FEATURES - 1) // 2
PAIRS = FEATURES * SHIFTS
PAIR_CHUNKS = 3
PAIR_ROWS = PAIRS // PAIR_CHUNKS
WIDE = FEATURES + SHIFTS

E_UNITS = (FEATURES + 1) // 2
E_BANKS = 2
ONEHOT_UNITS = NOH // 2
ROW_UNITS = E_UNITS - ONEHOT_UNITS


def unit_order():
    order, row = [], ONEHOT_UNITS
    for u in range(ONEHOT_UNITS):
        until = ONEHOT_UNITS + ROW_UNITS * (u + 1) // ONEHOT_UNITS
        order += [u, *range(row, until)]
        row = until
    return order


UNIT_ORDER = unit_order()
GRAM_GROUPS = 4
GRAM_UNITS = QUADS // GRAM_GROUPS
GRAM_BANKS = 4
HALVES = 2
OH_UNITS = NOH * HALVES
OH_SLOTS = 8
OH_AHEAD = 8
ID_UNITS = NOH // 2
Z_STORES, Z_REORDERS = 2, 4


def pair_rows():
    number = {}
    for a in range(FEATURES):
        for b in range(a + 1, FEATURES):
            number[a, b] = len(number)
    rows = []
    for i in range(FEATURES):
        for k in range(1, SHIFTS + 1):
            a, b = FEATURE_AT[i], FEATURE_AT[(i + k) % FEATURES]
            rows.append(number[min(a, b), max(a, b)])
    return rows


def dlrm_tower(nc, x, ids, ids_t, tables, w1_pairs, w1_dense, b1, w2, b2, w3, y):
    fp32, fp32r, i32 = mybir.dt.float32, mybir.dt.float32r, mybir.dt.int32
    ALU, ACT = mybir.AluOpType, mybir.ActivationFunctionType

    ctx = ExitStack()
    with ctx:
        def sb(name, shape, dt=fp32):
            return ctx.enter_context(nc.sbuf_tensor(name, shape, dt))

        def pb(name):
            return ctx.enter_context(nc.psum_tensor(name, [128, 512], fp32))

        def sem(name):
            return ctx.enter_context(nc.semaphore(name))

        table_hi = sb("table_hi", [SMALL_PARTS, CHUNK0[NOH], D], fp32r)
        table_lo = sb("table_lo", [SMALL_PARTS, CHUNK0[NOH], D], fp32r)
        onehot = sb("onehot", [SMALL_PARTS, OH_SLOTS, MAX_CHUNKS // 2, BATCH], fp32r)
        ids_row = sb("ids_row", [SMALL_PARTS, NOH, BATCH], i32)
        row_number = sb("row_number", [SMALL_PARTS, 18])
        row_int = sb("row_int", [SMALL_PARTS, 18], i32)
        gather_ids = sb("gather_ids", [TILE, 2, TILES, NG], i32)
        gathered = sb("gathered", [TILE, 2 * TILES, NG, D])
        dense_rows = sb("dense_rows", [TILE, 2, TILES, D])
        ident = sb("ident", [128, 128])
        E = sb("E", [D, BATCH, QUAD_ROWS])
        dense_t = sb("dense_t", [D, 2, BATCH])
        gram_sb = sb("gram_sb", [128, FEATURES, QUADS])
        pairs_t = sb("pairs_t", [PAIR_ROWS, PAIR_CHUNKS, BATCH])
        w1_sb = sb("w1_sb", [128, PAIR_CHUNKS + 1, H1])
        w2_sb = sb("w2_sb", [128, H1 // 128, H2])
        w3_sb = sb("w3_sb", [128, H2 // 128])
        b1_sb = sb("b1_sb", [128, H1 // 128])
        b2_sb = sb("b2_sb", [128, H2 // 128])
        h1_sb = sb("h1_sb", [128, H1 // 128, BATCH])
        h2_sb = sb("h2_sb", [128, H2 // 128, BATCH])
        y_sb = sb("y_sb", [1, BATCH])
        raw = [gathered[0:SMALL_PARTS, TILES + r, 0:MAX_CHUNKS, :] for r in range(2)]

        gram_dram = nc.dram_tensor("gram_dram", [128, WIDE, QUADS], fp32, kind="Internal").ap()
        pairs_dram = nc.dram_tensor("pairs_dram", [PAIRS, 4, QUADS], fp32, kind="Internal").ap()

        fill_ps = [pb(f"fill_ps{n}") for n in range(E_BANKS)]
        gram_ps = [pb(f"gram_ps{n}") for n in range(GRAM_BANKS)]
        mlp_ps = [pb(f"mlp_ps{n}") for n in range(2)]

        sp_waits = sem("sp_waits")
        pool_waits = sem("pool_waits")
        const_step = sem("const_step")
        consts_ready = sem("consts_ready")
        rows_ready = sem("rows_ready")
        weights_loaded = sem("weights_loaded")
        raw_loaded = [sem(f"raw_loaded{r}") for r in range(2)]
        hi_ready = sem("hi_ready")
        lo_ready = sem("lo_ready")
        gather_ids_loaded = [sem(f"gather_ids_loaded{p}") for p in range(2)]
        dense_loaded = [sem(f"dense_loaded{p}") for p in range(2)]
        ids_loaded = [sem(f"ids_loaded{m}") for m in range(ID_UNITS)]
        rows_gathered = [sem(f"rows_gathered{s}") for s in range(2 * TILES)]
        onehot_ready = sem("onehot_ready")
        onehot_used = sem("onehot_used")
        transposed = sem("transposed")
        E_ready = sem("E_ready")
        gram_done = sem("gram_done")
        gram_copied_act = sem("gram_copied_act")
        gram_copied_dve = sem("gram_copied_dve")
        gram_stored = sem("gram_stored")
        pairs_reordered = sem("pairs_reordered")
        pairs_loaded = sem("pairs_loaded")
        l1_done = sem("l1_done")
        h1_ready = sem("h1_ready")
        l2_done = sem("l2_done")
        h2_ready = sem("h2_ready")
        l3_done = sem("l3_done")
        y_ready = sem("y_ready")
        y_stored = sem("y_stored")

        block = ctx.enter_context(nc.Block())

        def batches(eng, step):
            step(0, 0, 0)
            with eng.Fori(0, (BATCHES - 2) // 2) as i:
                step(2 * i + 1, 1, i)
                step(2 * i + 2, 0, i + 1)
            step(BATCHES - 1, 1, BATCHES // 2 - 1)

        def samples_of(b):
            return bass.ds(b * BATCH, BATCH)

        def copy_gram(copy, w, q):
            src = gram_ps[w % GRAM_BANKS][32 * q:32 * q + 32, 0:GRAM_GROUPS * 4 * FEATURES]\
                .rearrange("i (g q j) -> i g q j", g=GRAM_GROUPS, q=4)[:, :, q, :]
            dst = gram_sb[32 * q:32 * q + 32, :, w * GRAM_GROUPS:(w + 1) * GRAM_GROUPS]
            return copy(dst, src.rearrange("i g j -> i j g"))

        @block.sync
        def _(sp):
            def load_batch_inputs(b, parity):
                sp.dma_start(gather_ids[:, parity, :, :],
                             ids[samples_of(b), :].rearrange("(t p) n -> p t n", p=TILE))\
                  .then_inc(gather_ids_loaded[parity], 16)
                sp.dma_start(dense_rows[:, parity, :, :],
                             x[samples_of(b), :].rearrange("(t p) d -> p t d", p=TILE))\
                  .then_inc(dense_loaded[parity], 16)

            def load_ids(b, m):
                src = ids_t[2 * m:2 * m + 2, samples_of(b)].unsqueeze(0)
                sp.dma_start(ids_row[:, 2 * m:2 * m + 2, :], src.to_broadcast([SMALL_PARTS, 2, BATCH]))\
                  .then_inc(ids_loaded[m], 16)

            def load_table(n):
                c = CHUNKS[n]
                sp.dma_start(raw[n % 2][:, 0:c, :], tables[n].rearrange("(p c) d -> p c d", c=c))\
                  .then_inc(raw_loaded[n % 2], 16)

            load_batch_inputs(0, 0)
            for n in range(NOH):
                if n >= 2:
                    sp.wait_ge(lo_ready, n - 1)
                load_table(n)
                if n % 2 == 0:
                    load_ids(0, n // 2)
                if n == 3:
                    load_batch_inputs(1, 1)
                    for dst, src in ((w1_sb[0:PAIR_ROWS, 0:PAIR_CHUNKS, :], w1_pairs.rearrange("c p n -> p c n")),
                                     (w1_sb[:, PAIR_CHUNKS, :], w1_dense),
                                     (w2_sb[:, :, :], w2.rearrange("(c p) n -> p c n", p=128)),
                                     (w3_sb[:, :], w3), (b1_sb[:, :], b1), (b2_sb[:, :], b2)):
                        sp.dma_start(dst, src).then_inc(weights_loaded, 16)

            def wait_for(semaphore, value):
                sp.wait_ge(semaphore, value)
                sp.sem_inc(sp_waits, 1)

            def step(b, parity, visit):
                first = isinstance(b, int) and b == 0
                last = isinstance(b, int) and b == BATCHES - 1
                if not first:
                    if not last:
                        for t in range(TILES):
                            wait_for(rows_gathered[(1 - parity) * TILES + t],
                                       (visit + parity) * NG * 16)
                        wait_for(transposed, 1 + b * ROW_UNITS)
                        load_batch_inputs(b + 1, 1 - parity)
                if not last:
                    for m in range(ID_UNITS):
                        wait_for(onehot_ready, b * OH_UNITS + 4 * (m + 1))
                        load_ids(b + 1, m)
                if not first:
                    wait_for(y_ready, b)
                    sp.dma_start(y[samples_of(b - 1)].unsqueeze(0), y_sb[:, :]).then_inc(y_stored, 16)
                    wait_for(pairs_loaded, b * 16)
                wait_for(gram_copied_act, (b + 1) * GRAM_UNITS)
                wait_for(gram_copied_dve, (b + 1) * GRAM_UNITS)
                sp.dma_start(gram_dram[:, 0:FEATURES, :], gram_sb[:, :, :]).then_inc(gram_stored, 16)
                sp.dma_start(gram_dram[:, FEATURES:WIDE, :], gram_sb[:, 0:SHIFTS, :]).then_inc(gram_stored, 16)
                wait_for(gram_stored, (b + 1) * Z_STORES * 16)
                for q in range(4):
                    src = bass.AP(gram_dram.tensor, (32 * q * WIDE + 1) * QUADS,
                                  [[(WIDE + 1) * QUADS, FEATURES], [QUADS, SHIFTS], [1, QUADS]])
                    sp.dma_start(pairs_dram[:, q, :].rearrange("(i k) g -> i k g", k=SHIFTS), src)\
                      .then_inc(pairs_reordered, 16)
                wait_for(pairs_reordered, (b + 1) * Z_REORDERS * 16)
                sp.dma_start(pairs_t[:, :, :],
                             pairs_dram.rearrange("(c r) q g -> r c (q g)", c=PAIR_CHUNKS))\
                  .then_inc(pairs_loaded, 16)

            batches(sp, step)
            sp.wait_ge(y_ready, BATCHES)
            sp.dma_start(y[samples_of(BATCHES - 1)].unsqueeze(0), y_sb[:, :]).then_inc(y_stored, 16)
            sp.wait_ge(y_stored, BATCHES * 16)

        @block.gpsimd
        def _(pool):
            pool.sem_inc(transposed, 1)
            pool.iota(row_int[:, 0:8], pattern=[[1, 8]], base=0, channel_multiplier=8).then_inc(const_step, 1)
            pool.iota(row_int[:, 8:18], pattern=[[1, 10]], base=0, channel_multiplier=10).then_inc(const_step, 1)
            pool.memset(ident[:, :], 0.0).then_inc(const_step, 1)
            pool.memset(E[:, :, FEATURES:QUAD_ROWS], 0.0).then_inc(const_step, 1)
            pool.wait_ge(const_step, 4)
            pool.tensor_copy(row_number[:, :], row_int[:, :]).then_inc(rows_ready, 1)
            pool.affine_select(out=ident[:, :], in_=ident[:, :], compare_op=ALU.not_equal, fill=1.0,
                               base=0, pattern=[[-1, 128]], channel_multiplier=1).then_inc(consts_ready, 1)

            def step(b, parity, visit):
                if not (isinstance(b, int) and b == 0):
                    pool.wait_ge(lo_ready, NOH)
                    pool.wait_ge(transposed, 1 + (b - 1) * ROW_UNITS)
                pool.wait_ge(gather_ids_loaded[parity], (visit + 1) * 16)
                pool.sem_inc(pool_waits, 1)
                for t in range(TILES):
                    for n, f in enumerate(GATHERED):
                        pool.indirect_dma_start(
                            out=gathered[:, parity * TILES + t, n, :], out_offset=None,
                            in_=tables[NOH + n],
                            in_offset=bass.IndirectOffsetOnAxis(ap=gather_ids[:, parity, t, n:n + 1], axis=0),
                        ).then_inc(rows_gathered[parity * TILES + t], 16)

            batches(pool, step)

        @block.scalar
        def _(act):
            def take_hi(n):
                act.wait_ge(raw_loaded[n % 2], (n // 2 + 1) * 16)
                nc.scalar.activation(table_hi[:, CHUNK0[n]:CHUNK0[n + 1], :], raw[n % 2][:, 0:CHUNKS[n], :],
                                     ACT.Copy).then_inc(hi_ready, 1)

            def relu1(b):
                for u in range(H1 // 128):
                    if u % 2 == 0:
                        act.wait_ge(l1_done, 2 * b + u // 2 + 1)
                    nc.scalar.activation(h1_sb[:, u, :], mlp_ps[u // 2][:, (u % 2) * BATCH:(u % 2 + 1) * BATCH],
                                         ACT.Relu, bias=b1_sb[:, u:u + 1]).then_inc(h1_ready, 1)

            def relu2(b):
                act.wait_ge(l2_done, b + 1)
                for m in range(H2 // 128):
                    nc.scalar.activation(h2_sb[:, m, :], mlp_ps[0][:, m * BATCH:(m + 1) * BATCH],
                                         ACT.Relu, bias=b2_sb[:, m:m + 1]).then_inc(h2_ready, 1)

            def copy_y(b):
                act.wait_ge(l3_done, b + 1)
                if not (isinstance(b, int) and b == 0):
                    act.wait_ge(y_stored, 16 * b)
                nc.scalar.activation(y_sb[:, :].rearrange("o (g q) -> o q g", q=4),
                                     mlp_ps[1][0:1, 0:BATCH].rearrange("o (q g) -> o q g", q=4),
                                     ACT.Copy).then_inc(y_ready, 1)

            def step(b, parity, visit):
                first = isinstance(b, int) and b == 0
                for k, u in enumerate(UNIT_ORDER):
                    if u < ONEHOT_UNITS:
                        act.wait_ge(onehot_used, b * OH_UNITS + (u + 1) * 2 * HALVES)
                    else:
                        act.wait_ge(transposed, 1 + b * ROW_UNITS + u - ONEHOT_UNITS + 1)
                    src = fill_ps[k % E_BANKS]
                    if u < E_UNITS - 1:
                        nc.scalar.activation(E[:, :, 2 * u:2 * u + 2].rearrange("d s f -> d f s"),
                                             src[:, :].rearrange("d (f s) -> d f s", f=2),
                                             ACT.Copy).then_inc(E_ready, 1)
                    else:
                        nc.scalar.activation(E[:, :, FEATURES - 1], src[:, 0:BATCH], ACT.Copy)
                        nc.scalar.activation(dense_t[:, parity, :].rearrange("d (q g) -> d q g", q=4),
                                             src[:, 0:BATCH].rearrange("d (g q) -> d q g", q=4),
                                             ACT.Copy).then_inc(E_ready, 1)
                if first:
                    act.wait_ge(weights_loaded, 6 * 16)
                else:
                    relu1(b - 1)
                for w in range(GRAM_UNITS):
                    act.wait_ge(gram_done, b * GRAM_UNITS + w + 1)
                    if w == 0 and not first:
                        act.wait_ge(gram_stored, b * Z_STORES * 16)
                    for q in (0, 1):
                        inst = copy_gram(nc.scalar.copy, w, q)
                    inst.then_inc(gram_copied_act, 1)
                    if not first and w == 6:
                        relu2(b - 1)
                    if not first and w == 11:
                        copy_y(b - 1)

            for n in range(NOH):
                take_hi(n)
            batches(act, step)
            relu1(BATCHES - 1)
            relu2(BATCHES - 1)
            copy_y(BATCHES - 1)

        @block.vector
        def _(dve):
            def take_lo(n):
                dve.wait_ge(hi_ready, n + 1)
                part = slice(CHUNK0[n], CHUNK0[n + 1])
                nc.vector.tensor_tensor(table_lo[:, part, :], raw[n % 2][:, 0:CHUNKS[n], :],
                                        table_hi[:, part, :].bitcast(fp32), ALU.subtract).then_inc(lo_ready, 1)

            def make_onehot(b, u):
                n, h = u // HALVES, u % HALVES
                if u % (2 * HALVES) == 0:
                    dve.wait_ge(ids_loaded[n // 2], 16 * (b + 1))
                if not (isinstance(b, int) and b == 0 and u < OH_SLOTS):
                    dve.wait_ge(onehot_used, b * OH_UNITS + u - OH_SLOTS + 1)
                half = CHUNKS[n] // HALVES
                for c in range(half):
                    col = (0 if CHUNKS[n] == 8 else 8) + h * half + c
                    inst = nc.vector.tensor_scalar(onehot[:, u % OH_SLOTS, c, :], ids_row[:, n, :],
                                                   row_number[:, col:col + 1], None, ALU.is_equal)
                inst.then_inc(onehot_ready, 1)

            def step(b, parity, visit):
                first = isinstance(b, int) and b == 0
                last = isinstance(b, int) and b == BATCHES - 1
                for u in range(OH_AHEAD, OH_UNITS):
                    make_onehot(b, u)
                for w in range(GRAM_UNITS):
                    dve.wait_ge(gram_done, b * GRAM_UNITS + w + 1)
                    if w == 0 and not first:
                        dve.wait_ge(gram_stored, b * Z_STORES * 16)
                    for q in (2, 3):
                        inst = copy_gram(nc.vector.tensor_copy, w, q)
                    inst.then_inc(gram_copied_dve, 1)
                    if w % 2 == 1 and w // 2 < OH_AHEAD and not last:
                        make_onehot(b + 1, w // 2)

            dve.wait_ge(rows_ready, 1)
            for n in range(NOH):
                take_lo(n)
                for u in range(n * HALVES, min((n + 1) * HALVES, OH_AHEAD)):
                    make_onehot(0, u)
            batches(dve, step)

        @block.tensor
        def _(pe):
            def fill(b, parity, visit):
                first = isinstance(b, int) and b == 0
                for k, u in enumerate(UNIT_ORDER):
                    out = fill_ps[k % E_BANKS]
                    if not (first and k < E_BANKS):
                        pe.wait_ge(E_ready, b * E_UNITS + k - E_BANKS + 1)
                    for pos in range(2 * u, min(2 * u + 2, FEATURES)):
                        cols = out[:, (pos % 2) * BATCH:(pos % 2 + 1) * BATCH]
                        if pos < NOH:
                            if first:
                                pe.wait_ge(lo_ready, pos + 1)
                            half = CHUNKS[pos] // HALVES
                            for h in range(HALVES):
                                s = pos * HALVES + h
                                pe.wait_ge(onehot_ready, b * OH_UNITS + s + 1)
                                for c in range(half):
                                    at = CHUNK0[pos] + h * half + c
                                    for part in (table_hi, table_lo):
                                        inst = nc.tensor.matmul(
                                            cols, part[:, at, :], onehot[:, s % OH_SLOTS, c, :],
                                            start=(h == 0 and c == 0 and part is table_hi),
                                            stop=(h == 1 and c == half - 1 and part is table_lo))
                                inst.then_inc(onehot_used, 1)
                        else:
                            for t in range(TILES):
                                if pos == FEATURES - 1:
                                    if t == 0:
                                        pe.wait_ge(dense_loaded[parity], (visit + 1) * 16)
                                    rows = dense_rows[:, parity, t, :]
                                else:
                                    if pos == NOH:
                                        pe.wait_ge(rows_gathered[parity * TILES + t], (visit + 1) * NG * 16)
                                    rows = gathered[:, parity * TILES + t, pos - NOH, :]
                                inst = nc.tensor.transpose(cols[:, t * TILE:(t + 1) * TILE], rows, ident[:, :])
                    if u >= ONEHOT_UNITS:
                        inst.then_inc(transposed, 1)

            def layer1(b, parity):
                pe.wait_ge(pairs_loaded, 16 * (b + 1))
                if not (isinstance(b, int) and b == 0):
                    pe.wait_ge(h2_ready, 2 * b)
                    pe.wait_ge(y_ready, b)
                for u in range(H1 // 128):
                    cols = mlp_ps[u // 2][:, (u % 2) * BATCH:(u % 2 + 1) * BATCH]
                    for c in range(PAIR_CHUNKS):
                        nc.tensor.matmul(cols, w1_sb[0:PAIR_ROWS, c, u * 128:(u + 1) * 128],
                                         pairs_t[:, c, :], start=(c == 0), stop=False)
                    inst = nc.tensor.matmul(cols, w1_sb[:, PAIR_CHUNKS, u * 128:(u + 1) * 128],
                                            dense_t[:, parity, :], start=False, stop=True)
                    if u % 2 == 1:
                        inst.then_inc(l1_done, 1)

            def layer2(b):
                pe.wait_ge(h1_ready, 4 * (b + 1))
                for m in range(H2 // 128):
                    for u in range(H1 // 128):
                        inst = nc.tensor.matmul(mlp_ps[0][:, m * BATCH:(m + 1) * BATCH],
                                                w2_sb[:, u, m * 128:(m + 1) * 128], h1_sb[:, u, :],
                                                start=(u == 0), stop=(u == H1 // 128 - 1))
                inst.then_inc(l2_done, 1)

            def layer3(b):
                pe.wait_ge(h2_ready, 2 * (b + 1))
                for m in range(H2 // 128):
                    inst = nc.tensor.matmul(mlp_ps[1][0:1, 0:BATCH], w3_sb[:, m:m + 1], h2_sb[:, m, :],
                                            start=(m == 0), stop=(m == H2 // 128 - 1))
                inst.then_inc(l3_done, 1)

            def step(b, parity, visit):
                first = isinstance(b, int) and b == 0
                fill(b, parity, visit)
                if first:
                    pe.wait_ge(weights_loaded, 6 * 16)
                else:
                    layer1(b - 1, 1 - parity)
                pe.wait_ge(E_ready, (b + 1) * E_UNITS)
                for w in range(GRAM_UNITS):
                    if not (first and w < GRAM_BANKS):
                        pe.wait_ge(gram_copied_act, b * GRAM_UNITS + w - GRAM_BANKS + 1)
                        pe.wait_ge(gram_copied_dve, b * GRAM_UNITS + w - GRAM_BANKS + 1)
                    for gg in range(GRAM_GROUPS):
                        g = w * GRAM_GROUPS + gg
                        four = E[:, 4 * g:4 * g + 4, :]
                        inst = nc.tensor.matmul(
                            gram_ps[w % GRAM_BANKS][:, gg * 4 * FEATURES:(gg + 1) * 4 * FEATURES],
                            four.rearrange("d s f -> d (s f)"), four[:, :, 0:FEATURES], start=True, stop=True)
                    inst.then_inc(gram_done, 1)
                    if not first and w == 4:
                        layer2(b - 1)
                    if not first and w == 9:
                        layer3(b - 1)

            pe.wait_ge(consts_ready, 1)
            pe.wait_ge(const_step, 4)
            batches(pe, step)
            layer1(BATCHES - 1, 1)
            layer2(BATCHES - 1)
            layer3(BATCHES - 1)


def kernel(**inputs):
    import concourse.bacc as _bacc
    from concourse.bass_utils import run_bass_kernel_spmd as _run

    nc = _bacc.Bacc("TRN2", target_bir_lowering=False, num_devices=1)
    ids = np.asarray(inputs["ids"])
    w1 = np.asarray(inputs["W_top1"])
    arrays = {
        "x": np.asarray(inputs["r_dense_x"]),
        "ids": np.ascontiguousarray(ids[:, GATHERED]),
        "ids_t": np.ascontiguousarray(ids[:, ONEHOT].T),
    }
    for n, f in enumerate(ONEHOT + GATHERED):
        arrays[f"table_{n}"] = np.asarray(inputs[f"tbl_{f}"])
    arrays["w1_pairs"] = np.ascontiguousarray(w1[pair_rows()]).reshape(PAIR_CHUNKS, PAIR_ROWS, H1)
    arrays["w1_dense"] = np.ascontiguousarray(w1[PAIRS:])
    arrays["b1"] = np.ascontiguousarray(np.asarray(inputs["b_top1"]).reshape(-1, 128).T)
    arrays["w2"] = np.asarray(inputs["W_top2"])
    arrays["b2"] = np.ascontiguousarray(np.asarray(inputs["b_top2"]).reshape(-1, 128).T)
    arrays["w3"] = np.ascontiguousarray(np.asarray(inputs["W_top3"]).reshape(-1, 128).T)
    aps = {k: nc.dram_tensor(f"{k}_in", a.shape, mybir.dt.from_np(a.dtype), kind="ExternalInput").ap()
           for k, a in arrays.items()}
    y = nc.dram_tensor("y_out", (SAMPLES,), mybir.dt.float32, kind="ExternalOutput").ap()
    tables = [aps[f"table_{n}"] for n in range(TABLES)]
    dlrm_tower(nc, aps["x"], aps["ids"], aps["ids_t"], tables, aps["w1_pairs"], aps["w1_dense"],
               aps["b1"], aps["w2"], aps["b2"], aps["w3"], y)
    got = _run(nc, [{f"{k}_in": a for k, a in arrays.items()}], core_ids=[0])
    return got.results[0]["y_out"].reshape(SAMPLES, 1)
```

```python
import numpy as np
import concourse.bass as bass
from concourse import mybir
from contextlib import ExitStack

TABLES = 26
FEATURES = TABLES + 1
D = 128
SAMPLES = 2048
H1, H2 = 512, 256
SMALL_PARTS = 125

BATCH = 256
HALF = BATCH // 2
BATCHES = (SAMPLES - 2 * HALF) // BATCH + 2
LAST = BATCHES - 1
PADDED = SAMPLES + HALF
TILE = 128
TILES = BATCH // TILE
QUADS = BATCH // 4

TABLE_ROWS = [1000, 1250, 125000, 1250, 1250, 12500, 1000, 1250, 1250, 1250, 1250, 1000, 1250,
              1000, 1000, 1000, 1000, 1250, 12500, 12500, 1000, 12500, 12500, 1250, 1000, 1000]
ONEHOT_COUNT = 8
ONEHOT = sorted((f for f in range(TABLES) if TABLE_ROWS[f] <= 1250),
                key=lambda f: (TABLE_ROWS[f], f))[:ONEHOT_COUNT]
GATHERED = [f for f in range(TABLES) if f not in ONEHOT]
NOH, NG = len(ONEHOT), len(GATHERED)
LAST_ONEHOT = 2
LAST_EXTRA = ONEHOT[LAST_ONEHOT:]
FEATURE_AT = [f for pair in zip(ONEHOT, GATHERED) for f in pair] + GATHERED[NOH:] + [TABLES]
assert all(TABLE_ROWS[f] == 1000 for f in ONEHOT)
CHUNKS = TABLE_ROWS[ONEHOT[0]] // SMALL_PARTS

SHIFTS = (FEATURES - 1) // 2
PAIRS = FEATURES * SHIFTS
PAIR_CHUNKS = 3
PAIR_ROWS = PAIRS // PAIR_CHUNKS
WIDE = FEATURES + SHIFTS

E_UNITS = (FEATURES + 1) // 2
FILL_BANKS = 4


def unit_order():
    order, other = [], NOH
    for u in range(NOH):
        until = NOH + (E_UNITS - NOH) * (u + 1) // NOH
        order += [u, *range(other, until)]
        other = until
    return order




FIRST_ORDER = list(range(E_UNITS))
INPUT_SPLIT_AT = 10
LAYER2_AT, RELU2_AT, LAYER3_AT, COPY_Y_AT = 2, 0, 5, 6
UNIT_ORDER = unit_order()


def bank_of(u, first):
    if u < NOH:
        return u if first else u % 2
    return 2 + u % 2


def bank_freed_by(order, k, first):
    earlier = [j for j in range(k) if bank_of(order[j], first) == bank_of(order[k], first)]
    return earlier[-1] + 1 if earlier else 0
GRAM_GROUPS = 4
GRAM_UNITS_OF = {n: n // 4 // GRAM_GROUPS for n in (HALF, BATCH)}
GRAM_BANKS = 4
HALVES = 2
BLOCK_CHUNKS = CHUNKS // HALVES
OH_UNITS = NOH * HALVES
OH_SLOTS = 4
OH_AHEAD = LAST_ONEHOT * HALVES
RAW_IN_E = BATCH * FEATURES // (CHUNKS * D)
WARM = (30, 12, 14, 8)
BLOCKS_AT = {HALF: (1, 3, 5, 7), BATCH: (3, 7, 9, 13)}
ID_UNITS = NOH // 2
Z_STORES, Z_REORDERS = 2, 4


def pair_rows():
    number = {}
    for a in range(FEATURES):
        for b in range(a + 1, FEATURES):
            number[a, b] = len(number)
    rows = []
    for i in range(FEATURES):
        for k in range(1, SHIFTS + 1):
            a, b = FEATURE_AT[i], FEATURE_AT[(i + k) % FEATURES]
            rows.append(number[min(a, b), max(a, b)])
    return rows


def dlrm_tower(nc, x, ids, ids_t, tables, w1_pairs, w1_dense, b1, w2, b2, w3, y):
    fp32, fp32r, i32 = mybir.dt.float32, mybir.dt.float32r, mybir.dt.int32
    ALU, ACT = mybir.AluOpType, mybir.ActivationFunctionType

    ctx = ExitStack()
    with ctx:
        def sb(name, shape, dt=fp32):
            return ctx.enter_context(nc.sbuf_tensor(name, shape, dt))

        def pb(name):
            return ctx.enter_context(nc.psum_tensor(name, [128, 512], fp32))

        def sem(name):
            return ctx.enter_context(nc.semaphore(name))

        table_hi = sb("table_hi", [SMALL_PARTS, NOH * CHUNKS, D], fp32r)
        table_lo = sb("table_lo", [SMALL_PARTS, NOH * CHUNKS, D], fp32r)
        onehot = sb("onehot", [SMALL_PARTS, OH_SLOTS, BLOCK_CHUNKS, BATCH], fp32r)
        ids_row = sb("ids_row", [SMALL_PARTS, NOH, BATCH], i32)
        row_number = sb("row_number", [SMALL_PARTS, CHUNKS])
        row_int = sb("row_int", [SMALL_PARTS, CHUNKS], i32)
        all_ids = sb("all_ids", [TILE, SAMPLES // TILE, NG], i32)
        extra_ids = sb("extra_ids", [TILE, len(LAST_EXTRA)], i32)
        gather_ids = sb("gather_ids", [TILE, 2, TILES, NG], i32)
        gathered = sb("gathered", [TILE, 2 * TILES, NG, D])
        dense_rows = sb("dense_rows", [TILE, 2, TILES, D])
        ident = sb("ident", [128, 128])
        E = sb("E", [D, BATCH, FEATURES])
        dense_t = sb("dense_t", [D, 2, BATCH])
        gram_sb = sb("gram_sb", [128, FEATURES * QUADS])
        pairs_t = sb("pairs_t", [PAIR_ROWS, PAIR_CHUNKS, BATCH])
        w1_hi = sb("w1_hi", [128, PAIR_CHUNKS + 1, H1], fp32r)
        w1_lo = sb("w1_lo", [128, PAIR_CHUNKS + 1, H1], fp32r)
        in_hi = sb("in_hi", [128, PAIR_CHUNKS + 1, BATCH], fp32r)
        in_lo = sb("in_lo", [128, PAIR_CHUNKS + 1, BATCH], fp32r)
        w2_hi = sb("w2_hi", [128, H1 // 128, H2], fp32r)
        w2_lo = sb("w2_lo", [128, H1 // 128, H2], fp32r)
        w3_sb = sb("w3_sb", [128, H2 // 128])
        b1_sb = sb("b1_sb", [128, H1 // 128])
        b2_sb = sb("b2_sb", [128, H2 // 128])
        h1_sb = sb("h1_sb", [128, H1 // 128, BATCH])
        h2_sb = sb("h2_sb", [128, H2 // 128, BATCH])
        y_cols = sb("y_cols", [TILE, SAMPLES // TILE])
        y_rows = sb("y_rows", [SAMPLES // TILE, TILE])
        in_E = [E[:, :, :].rearrange("p s f -> p (s f)")[:, n * CHUNKS * D:(n + 1) * CHUNKS * D]
                for n in range(RAW_IN_E)]
        raw_places = in_E + [gram_sb[:, n * CHUNKS * D:(n + 1) * CHUNKS * D]
                             for n in range(NOH - 1 - RAW_IN_E)]
        raw = [raw_places[n % len(raw_places)][0:SMALL_PARTS, :].rearrange("p (c d) -> p c d", d=D)
               for n in range(NOH)]
        raw_w1 = gathered[:, 1, 0:16, :].rearrange("p n d -> p (n d)").rearrange("p (c m) -> p c m", m=H1)
        raw_w2 = in_E[1].rearrange("p (c n) -> p c n", n=H2)
        table_part = [slice(n * CHUNKS, (n + 1) * CHUNKS) for n in range(NOH)]

        gram_dram = {n: nc.dram_tensor(f"gram_dram{n}", [4 * FEATURES, WIDE, n // 4], fp32, kind="Internal").ap()
                     for n in (HALF, BATCH)}
        pairs_dram = {n: nc.dram_tensor(f"pairs_dram{n}", [PAIRS, 4, n // 4], fp32, kind="Internal").ap()
                      for n in (HALF, BATCH)}

        fill_ps = [pb(f"fill_ps{n}") for n in range(FILL_BANKS)]
        gram_ps = [pb(f"gram_ps{n}") for n in range(GRAM_BANKS)]
        unit_ps = fill_ps + gram_ps

        def mlp_ps(b):
            return gram_ps if isinstance(b, int) and b == LAST else fill_ps

        sp_waits = sem("sp_waits")
        pool_waits = sem("pool_waits")
        const_step = sem("const_step")
        consts_ready = sem("consts_ready")
        rows_ready = sem("rows_ready")
        weights_loaded = sem("weights_loaded")
        raw_loaded = [sem(f"raw_loaded{n}") for n in range(NOH)]
        w2_loaded = sem("w2_loaded")
        w2_hi_ready = sem("w2_hi_ready")
        w2_lo_ready = sem("w2_lo_ready")
        w1_loaded = sem("w1_loaded")
        w1_hi_ready = sem("w1_hi_ready")
        w1_lo_ready = sem("w1_lo_ready")
        in_hi_ready = sem("in_hi_ready")
        in_lo_ready = sem("in_lo_ready")
        hi_ready = sem("hi_ready")
        lo_ready = sem("lo_ready")
        first_ids_loaded = sem("first_ids_loaded")
        other_ids_loaded = sem("other_ids_loaded")
        batch_ids_ready = sem("batch_ids_ready")
        dense_loaded = [sem(f"dense_loaded{p}") for p in range(2)]
        ids_loaded = [sem(f"ids_loaded{m}") for m in range(ID_UNITS)]
        rows_gathered = [sem(f"rows_gathered{s}") for s in range(2 * TILES)]
        onehot_ready = sem("onehot_ready")
        onehot_used = sem("onehot_used")
        filled = sem("filled")
        E_ready = sem("E_ready")
        gram_done = sem("gram_done")
        block_copied_act = sem("block_copied_act")
        block_copied_dve = sem("block_copied_dve")
        gram_copied_act = sem("gram_copied_act")
        gram_copied_dve = sem("gram_copied_dve")
        gram_stored = sem("gram_stored")
        pairs_reordered = sem("pairs_reordered")
        pairs_loaded = sem("pairs_loaded")
        l1_done = sem("l1_done")
        h1_ready = sem("h1_ready")
        h1_hi_ready = sem("h1_hi_ready")
        h1_lo_ready = sem("h1_lo_ready")
        l2_done = sem("l2_done")
        h2_ready = sem("h2_ready")
        l3_done = sem("l3_done")
        y_ready = sem("y_ready")
        y_transposed = sem("y_transposed")
        y_rows_ready = sem("y_rows_ready")
        y_stored = sem("y_stored")

        block = ctx.enter_context(nc.Block())

        def batches(eng, step):
            step(0, 0, 0, HALF)
            step(1, 1, 0, BATCH)
            with eng.Fori(0, (BATCHES - 3) // 2) as i:
                step(2 * i + 2, 0, i + 1, BATCH)
                step(2 * i + 3, 1, i + 1, BATCH)
            step(LAST, 0, LAST // 2, HALF)

        def first_sample(b):
            return 0 if is_number(b, 0) else b * BATCH - HALF

        def is_number(b, number):
            return isinstance(b, int) and b == number

        def before(b):
            return HALF if is_number(b, 1) else BATCH

        def gram_units_before(b):
            return 0 if is_number(b, 0) else b * GRAM_UNITS_OF[BATCH] - GRAM_UNITS_OF[HALF]

        def gathers_until(parity, t, visit):
            return (visit + (0 if parity == 0 and t == 1 else 1)) * NG * 16

        EXTRA_BEFORE = (LAST // 2 - 1) * NG * 16

        def gram_view(n):
            return gram_sb[:, 0:FEATURES * n // 4].rearrange("p (j g) -> p j g", j=FEATURES)

        def copy_gram(eng, copy, block_copied, b, w, n, meanwhile=None):
            unit = copied_before(b) + w // 2
            for q in (3, 2, 1, 0):
                if q < 3:
                    eng.wait_ge(block_copied, 3 * unit + 3 - q)
                rows = slice(0, (q + 1) * FEATURES)
                src = gram_ps[w % GRAM_BANKS][rows, 0:GRAM_GROUPS * 4 * FEATURES]\
                    .rearrange("i (g q j) -> i g q j", g=GRAM_GROUPS, q=4)[:, :, q, :]
                dst = gram_view(n)[rows, :, w * GRAM_GROUPS:(w + 1) * GRAM_GROUPS]
                inst = copy(dst, src.rearrange("i g j -> i j g"))
                if q > 0:
                    inst.then_inc(block_copied, 1)
                if meanwhile is not None and q > 0:
                    meanwhile(3 - q)
            return inst

        def copied_before(b):
            return 0 if is_number(b, 0) else b * (GRAM_UNITS_OF[BATCH] // 2) - GRAM_UNITS_OF[HALF] // 2

        w1_parts = [(slice(0, PAIR_ROWS), slice(0, PAIR_CHUNKS)), (slice(0, 128), slice(PAIR_CHUNKS, PAIR_CHUNKS + 1))]

        def input_parts(parity, n):
            return [(pairs_t[:, :, 0:n], *w1_parts[0]), (dense_t[:, parity:parity + 1, 0:n], *w1_parts[1])]

        @block.sync
        def _(sp):
            def load_dense(b, parity, tiles):
                src = x[bass.ds(first_sample(b), tiles * TILE), :].rearrange("(t p) d -> p t d", p=TILE)
                sp.dma_start(dense_rows[:, parity, 0:tiles, :], src).then_inc(dense_loaded[parity], 16)

            def load_ids(b, m, n):
                src = ids_t[2 * m:2 * m + 2, bass.ds(first_sample(b), n)].unsqueeze(0)
                sp.dma_start(ids_row[:, 2 * m:2 * m + 2, 0:n], src.to_broadcast([SMALL_PARTS, 2, n]))\
                  .then_inc(ids_loaded[m], 16)

            by_tile = ids.rearrange("(t p) n -> p t n", p=TILE)
            sp.dma_start(all_ids[:, 0:1, :], by_tile[:, 0:1, 0:NG]).then_inc(first_ids_loaded, 16)
            def load_table(n):
                sp.dma_start(raw[n], tables[n].rearrange("(p c) d -> p c d", c=CHUNKS))\
                  .then_inc(raw_loaded[n], 16)

            for n in range(NOH - 1):
                load_table(n)
                if n % 2 == 0:
                    load_ids(0, n // 2, HALF)
            sp.dma_start(raw_w1[0:PAIR_ROWS, 0:PAIR_CHUNKS, :], w1_pairs.rearrange("c p n -> p c n"))\
              .then_inc(w1_loaded, 16)
            sp.dma_start(raw_w1[:, PAIR_CHUNKS, :], w1_dense).then_inc(w1_loaded, 16)
            sp.dma_start(all_ids[:, 1:, :], by_tile[:, 1:, 0:NG]).then_inc(other_ids_loaded, 16)
            sp.dma_start(extra_ids[:, :], by_tile[:, SAMPLES // TILE - 1, NG:]).then_inc(other_ids_loaded, 16)
            load_dense(0, 0, 1)
            load_dense(1, 1, TILES)
            sp.wait_ge(lo_ready, 1)
            load_table(NOH - 1)
            sp.wait_ge(lo_ready, 2)
            sp.dma_start(raw_w2, w2.rearrange("(c p) n -> p c n", p=128)).then_inc(w2_loaded, 16)
            for dst, src in ((w3_sb[:, :], w3), (b1_sb[:, :], b1), (b2_sb[:, :], b2)):
                sp.dma_start(dst, src).then_inc(weights_loaded, 16)

            def wait_for(semaphore, value):
                sp.wait_ge(semaphore, value)
                sp.sem_inc(sp_waits, 1)

            def step(b, parity, visit, n):
                first, last = is_number(b, 0), is_number(b, LAST)
                quads = n // 4
                if not first and not last:
                    wait_for(filled, b * E_UNITS)
                    load_dense(b + 1, 1 - parity, TILES)
                if not last:
                    for m in range(ID_UNITS):
                        wait_for(onehot_ready, b * OH_UNITS + 4 * (m + 1))
                        load_ids(b + 1, m, BATCH)
                if not first:
                    wait_for(pairs_loaded, b * 16)
                wait_for(gram_copied_act, copied_before(b) + GRAM_UNITS_OF[n] // 2)
                wait_for(gram_copied_dve, copied_before(b) + GRAM_UNITS_OF[n] // 2)
                sp.dma_start(gram_dram[n][:, 0:FEATURES, :], gram_view(n)[0:4 * FEATURES, :, :]).then_inc(gram_stored, 16)
                sp.dma_start(gram_dram[n][:, FEATURES:WIDE, :], gram_view(n)[0:4 * FEATURES, 0:SHIFTS, :])\
                  .then_inc(gram_stored, 16)
                wait_for(gram_stored, (b + 1) * Z_STORES * 16)
                for q in range(4):
                    src = bass.AP(gram_dram[n].tensor, (FEATURES * q * WIDE + 1) * quads,
                                  [[(WIDE + 1) * quads, FEATURES], [quads, SHIFTS], [1, quads]])
                    sp.dma_start(pairs_dram[n][:, q, :].rearrange("(i k) g -> i k g", k=SHIFTS), src)\
                      .then_inc(pairs_reordered, 16)
                wait_for(pairs_reordered, (b + 1) * Z_REORDERS * 16)
                if last:
                    sp.wait_ge(in_lo_ready, LAST)
                sp.dma_start(pairs_t[:, :, 0:n], pairs_dram[n].rearrange("(c r) q g -> r c (q g)", c=PAIR_CHUNKS))\
                  .then_inc(pairs_loaded, 16)

            batches(sp, step)
            sp.wait_ge(y_rows_ready, 1)
            sp.dma_start(y.rearrange("(t p) -> t p", p=TILE), y_rows[:, :]).then_inc(y_stored, 16)
            sp.wait_ge(y_stored, 16)
            for m in range(LAST_ONEHOT // 2, ID_UNITS):
                sp.wait_ge(ids_loaded[m], BATCHES * 16)

        @block.gpsimd
        def _(pool):
            pool.iota(row_int[:, :], pattern=[[1, CHUNKS]], base=0, channel_multiplier=CHUNKS)\
                .then_inc(const_step, 1)
            pool.memset(ident[:, :], 0.0).then_inc(const_step, 1)
            pool.wait_ge(const_step, 2)
            pool.tensor_copy(row_number[:, :], row_int[:, :]).then_inc(rows_ready, 1)
            pool.affine_select(out=ident[:, :], in_=ident[:, :], compare_op=ALU.not_equal, fill=1.0,
                               base=0, pattern=[[-1, 128]], channel_multiplier=1).then_inc(consts_ready, 1)

            def step(b, parity, visit, n):
                tiles = n // TILE
                if is_number(b, 0):
                    pool.wait_ge(first_ids_loaded, 16)
                    ids_of_batch = all_ids[:, 0:1, :]
                else:
                    pool.wait_ge(other_ids_loaded, 2 * 16)
                    if not is_number(b, 1):
                        pool.wait_ge(filled, (b - 1) * E_UNITS)
                        pool.wait_ge(w1_lo_ready, 1)
                    ids_of_batch = all_ids[:, bass.ds(b * TILES - 1, tiles), :]
                pool.tensor_copy(gather_ids[:, parity, 0:tiles, :], ids_of_batch).then_inc(batch_ids_ready, 1)
                pool.wait_ge(batch_ids_ready, b + 1)
                pool.sem_inc(pool_waits, 1)
                for t in range(tiles):
                    for g in range(NG):
                        pool.indirect_dma_start(
                            out=gathered[:, parity * TILES + t, g, :], out_offset=None,
                            in_=tables[NOH + g],
                            in_offset=bass.IndirectOffsetOnAxis(ap=gather_ids[:, parity, t, g:g + 1], axis=0),
                        ).then_inc(rows_gathered[parity * TILES + t], 16)
                if is_number(b, LAST):
                    for g in range(len(LAST_EXTRA)):
                        pool.indirect_dma_start(
                            out=gathered[:, 1, g, :], out_offset=None, in_=tables[LAST_ONEHOT + g],
                            in_offset=bass.IndirectOffsetOnAxis(ap=extra_ids[:, g:g + 1], axis=0),
                        ).then_inc(rows_gathered[1], 16)

            batches(pool, step)

        @block.scalar
        def _(act):
            def take_hi(n):
                act.wait_ge(raw_loaded[n], 16)
                nc.scalar.activation(table_hi[:, table_part[n], :], raw[n], ACT.Copy).then_inc(hi_ready, 1)

            def take_input_hi(b, parity, n):
                if not is_number(b, 0):
                    act.wait_ge(l2_done, b)
                act.wait_ge(pairs_loaded, 16 * (b + 1))
                for src, rows, chunks in input_parts(parity, n):
                    inst = nc.scalar.activation(in_hi[rows, chunks, 0:n], src, ACT.Copy)
                inst.then_inc(in_hi_ready, 1)

            def relu1(b, n):
                def relu(half):
                    for u in (2 * half, 2 * half + 1):
                        columns = mlp_ps(b)[half][:, (u % 2) * BATCH:(u % 2) * BATCH + n]
                        nc.scalar.activation(h1_sb[:, u, 0:n], columns, ACT.Relu,
                                             bias=b1_sb[:, u:u + 1]).then_inc(h1_ready, 1)

                def take_hi(half):
                    part = slice(2 * half, 2 * half + 2)
                    act.wait_ge(h1_ready, 4 * b + 2 * half + 2)
                    nc.scalar.activation(in_hi[:, part, 0:n], h1_sb[:, part, 0:n], ACT.Copy).then_inc(h1_hi_ready, 1)

                act.wait_ge(l1_done, 2 * b + 1)
                relu(0)
                act.wait_ge(l1_done, 2 * b + 2)
                take_hi(0)
                relu(1)
                take_hi(1)

            def relu2(b, n):
                act.wait_ge(l2_done, b + 1)
                for m in range(H2 // 128):
                    nc.scalar.activation(h2_sb[:, m, 0:n].rearrange("p (g q) -> p q g", q=4),
                                         mlp_ps(b)[2 + m][:, 0:n].rearrange("p (q g) -> p q g", q=4),
                                         ACT.Relu, bias=b2_sb[:, m:m + 1]).then_inc(h2_ready, 1)

            def copy_y(b, n):
                act.wait_ge(l3_done, b + 1)
                tile = 0 if is_number(b, 0) else b * TILES - 1
                nc.scalar.activation(y_cols[:, bass.ds(tile, n // TILE)], mlp_ps(b)[1][:, 0:n // TILE],
                                     ACT.Copy).then_inc(y_ready, 1)

            def step(b, parity, visit, n):
                first, last = is_number(b, 0), is_number(b, LAST)
                for k, u in enumerate(FIRST_ORDER if first else UNIT_ORDER):
                    if k == INPUT_SPLIT_AT and not first and not last:
                        take_input_hi(b - 1, 1 - parity, before(b))
                    act.wait_ge(filled, b * E_UNITS + k + 1)
                    src = unit_ps[bank_of(u, first)]
                    if u < E_UNITS - 1:
                        nc.scalar.activation(E[:, 0:n, 2 * u:2 * u + 2].rearrange("d s f -> d f s"),
                                             src[:, :].rearrange("d (f s) -> d f s", f=2)[:, :, 0:n],
                                             ACT.Copy).then_inc(E_ready, 1)
                    else:
                        nc.scalar.activation(E[:, 0:n, FEATURES - 1], src[:, 0:n], ACT.Copy)
                        nc.scalar.activation(dense_t[:, parity, 0:n].rearrange("d (q g) -> d q g", q=4),
                                             src[:, 0:n].rearrange("d (g q) -> d q g", q=4),
                                             ACT.Copy).then_inc(E_ready, 1)
                if first:
                    act.wait_ge(weights_loaded, 3 * 16)
                elif not last:
                    relu1(b - 1, before(b))
                for w in range(0, GRAM_UNITS_OF[n], 2):
                    act.wait_ge(gram_done, gram_units_before(b) + w + 1)
                    if w == 0 and not first:
                        act.wait_ge(gram_stored, b * Z_STORES * 16)
                    copy_gram(act, nc.scalar.copy, block_copied_act, b, w, n).then_inc(gram_copied_act, 1)
                    if not first and not last and w == RELU2_AT:
                        relu2(b - 1, before(b))
                    if not first and not last and w == COPY_Y_AT:
                        copy_y(b - 1, before(b))

            for n in range(NOH):
                take_hi(n)
            act.wait_ge(w1_loaded, 2 * 16)
            for rows, chunks in w1_parts:
                inst = nc.scalar.activation(w1_hi[rows, chunks, :], raw_w1[rows, chunks, :], ACT.Copy)
            inst.then_inc(w1_hi_ready, 1)
            act.wait_ge(w2_loaded, 16)
            nc.scalar.activation(w2_hi[:, :, :], raw_w2, ACT.Copy).then_inc(w2_hi_ready, 1)
            act.wait_ge(lo_ready, NOH)
            act.wait_ge(w2_lo_ready, 1)
            batches(act, step)
            take_input_hi(LAST - 1, 1, BATCH)
            relu1(LAST - 1, BATCH)
            take_input_hi(LAST, 0, HALF)
            relu2(LAST - 1, BATCH)
            relu1(LAST, HALF)
            copy_y(LAST - 1, BATCH)
            relu2(LAST, HALF)
            copy_y(LAST, HALF)
            act.wait_ge(y_transposed, 1)
            nc.scalar.activation(y_rows[:, :], mlp_ps(LAST)[0][0:SAMPLES // TILE, 0:TILE], ACT.Copy).then_inc(y_rows_ready, 1)

        @block.vector
        def _(dve):
            def take_lo(n):
                dve.wait_ge(hi_ready, n + 1)
                part = table_part[n]
                nc.vector.tensor_tensor(table_lo[:, part, :], raw[n], table_hi[:, part, :].bitcast(fp32),
                                        ALU.subtract).then_inc(lo_ready, 1)

            def split_weights():
                dve.wait_ge(w1_hi_ready, 1)
                for rows, chunks in w1_parts:
                    inst = nc.vector.tensor_tensor(w1_lo[rows, chunks, :], raw_w1[rows, chunks, :],
                                                   w1_hi[rows, chunks, :].bitcast(fp32), ALU.subtract)
                inst.then_inc(w1_lo_ready, 1)
                dve.wait_ge(w2_hi_ready, 1)
                nc.vector.tensor_tensor(w2_lo[:, :, :], raw_w2, w2_hi[:, :, :].bitcast(fp32), ALU.subtract)\
                    .then_inc(w2_lo_ready, 1)

            def take_input_lo(b, parity, n):
                dve.wait_ge(in_hi_ready, b + 1)
                for src, rows, chunks in input_parts(parity, n):
                    inst = nc.vector.tensor_tensor(in_lo[rows, chunks, 0:n], src,
                                                   in_hi[rows, chunks, 0:n].bitcast(fp32), ALU.subtract)
                inst.then_inc(in_lo_ready, 1)

            def take_h1_lo(b, n):
                for half in range(2):
                    part = slice(2 * half, 2 * half + 2)
                    dve.wait_ge(h1_hi_ready, 2 * b + half + 1)
                    nc.vector.tensor_tensor(in_lo[:, part, 0:n], h1_sb[:, part, 0:n],
                                            in_hi[:, part, 0:n].bitcast(fp32), ALU.subtract).then_inc(h1_lo_ready, 1)

            def onehot_chunk(b, u, c, n):
                table, h = u // HALVES, u % HALVES
                if c == 0:
                    if u % (2 * HALVES) == 0:
                        dve.wait_ge(ids_loaded[table // 2], 16 * (b + 1))
                    if not (is_number(b, 0) and u < OH_SLOTS):
                        dve.wait_ge(onehot_used, b * OH_UNITS + u - OH_SLOTS + 1)
                col = h * BLOCK_CHUNKS + c
                inst = nc.vector.tensor_scalar(onehot[:, u % OH_SLOTS, c, 0:n], ids_row[:, table, 0:n],
                                               row_number[:, col:col + 1], None, ALU.is_equal)
                if c == BLOCK_CHUNKS - 1:
                    inst.then_inc(onehot_ready, 1)

            def make_onehot(b, u, n):
                for c in range(BLOCK_CHUNKS):
                    onehot_chunk(b, u, c, n)

            def step(b, parity, visit, n):
                first, last = is_number(b, 0), is_number(b, LAST)
                if not last:
                    for u in range(OH_AHEAD, OH_UNITS):
                        make_onehot(b, u, n)
                        if first and u == OH_AHEAD + OH_SLOTS - 1:
                            split_weights()
                if not first and not last:
                    take_input_lo(b - 1, 1 - parity, before(b))
                    take_h1_lo(b - 1, before(b))
                for w in range(1, GRAM_UNITS_OF[n], 2):
                    dve.wait_ge(gram_done, gram_units_before(b) + w + 1)
                    if w == 1 and not first:
                        dve.wait_ge(gram_stored, b * Z_STORES * 16)
                    block = BLOCKS_AT[n].index(w) if w in BLOCKS_AT[n] and not last else None
                    between = None if block is None else (lambda c: onehot_chunk(b + 1, block, c, BATCH))
                    copy_gram(dve, nc.vector.tensor_copy, block_copied_dve, b, w, n, between)\
                        .then_inc(gram_copied_dve, 1)
                    if block is not None:
                        onehot_chunk(b + 1, block, BLOCK_CHUNKS - 1, BATCH)

            dve.wait_ge(rows_ready, 1)
            for n in range(NOH):
                take_lo(n)
                for u in range(n * HALVES, min((n + 1) * HALVES, OH_AHEAD)):
                    make_onehot(0, u, HALF)
            batches(dve, step)
            take_input_lo(LAST - 1, 1, BATCH)
            take_h1_lo(LAST - 1, BATCH)
            take_input_lo(LAST, 0, HALF)
            take_h1_lo(LAST, HALF)

        @block.tensor
        def _(pe):
            def lookup(b, table, cols, n):
                if is_number(b, 0):
                    pe.wait_ge(lo_ready, table + 1)
                for h in range(HALVES):
                    block_number = table * HALVES + h
                    pe.wait_ge(onehot_ready, b * OH_UNITS + block_number + 1)
                    for c in range(BLOCK_CHUNKS):
                        for part in (table_hi, table_lo):
                            inst = nc.tensor.matmul(
                                cols, part[:, table * CHUNKS + h * BLOCK_CHUNKS + c, :],
                                onehot[:, block_number % OH_SLOTS, c, 0:n],
                                start=(h == 0 and c == 0 and part is table_hi),
                                stop=(h == 1 and c == BLOCK_CHUNKS - 1 and part is table_lo))
                    inst.then_inc(onehot_used, 1)
                return inst

            def columns(u, pos, first, n):
                at = (pos % 2) * BATCH
                return unit_ps[bank_of(u, first)][:, at:at + n]

            def transposed(cols, parity, pos, tiles):
                g = pos // 2 if pos < 2 * NOH else pos - NOH
                for t in range(tiles):
                    if pos == FEATURES - 1:
                        rows = dense_rows[:, parity, t, :]
                    elif pos < 2 * NOH and pos % 2 == 0:
                        rows = gathered[:, 1, pos // 2 - LAST_ONEHOT, :]
                    else:
                        rows = gathered[:, parity * TILES + t, g, :]
                    inst = nc.tensor.transpose(cols[:, t * TILE:(t + 1) * TILE], rows, ident[:, :])
                return inst

            def first_fill():
                for u in range(NOH):
                    lookup(0, u, columns(u, 2 * u, True, HALF), HALF)
                pe.wait_ge(rows_gathered[0], gathers_until(0, 0, 0))
                for u in range(NOH):
                    transposed(columns(u, 2 * u + 1, True, HALF), 0, 2 * u + 1, 1).then_inc(filled, 1)
                pe.wait_ge(dense_loaded[0], 16)
                for u in range(NOH, E_UNITS):
                    pe.wait_ge(E_ready, bank_freed_by(FIRST_ORDER, u, True))
                    for pos in range(2 * u, min(2 * u + 2, FEATURES)):
                        inst = transposed(columns(u, pos, True, HALF), 0, pos, 1)
                    inst.then_inc(filled, 1)

            def fill(b, parity, visit, n):
                tiles = n // TILE
                for k, u in enumerate(UNIT_ORDER):
                    freed = bank_freed_by(UNIT_ORDER, k, False)
                    if freed:
                        pe.wait_ge(E_ready, b * E_UNITS + freed)
                    by_lookup = u < (LAST_ONEHOT if is_number(b, LAST) else NOH)
                    if k == 0 and is_number(b, 1):
                        for early in UNIT_ORDER[0:2]:
                            lookup(b, early, columns(early, 2 * early, False, n), n)
                    elif by_lookup and not (k == 1 and is_number(b, 1)):
                        lookup(b, u, columns(u, 2 * u, False, n), n)
                    if k == 0:
                        for t in range(tiles):
                            pe.wait_ge(rows_gathered[parity * TILES + t], gathers_until(parity, t, visit))
                        if is_number(b, LAST):
                            pe.wait_ge(rows_gathered[1], EXTRA_BEFORE + 16 * len(LAST_EXTRA))
                    for pos in range(2 * u, min(2 * u + 2, FEATURES)):
                        if pos == FEATURES - 1:
                            pe.wait_ge(dense_loaded[parity], (visit + 1) * 16)
                        if not by_lookup or pos % 2 == 1:
                            inst = transposed(columns(u, pos, False, n), parity, pos, tiles)
                    inst.then_inc(filled, 1)

            def layer1(b, n, filled_after=None):
                pe.wait_ge(in_lo_ready, b + 1)
                for u in range(H1 // 128):
                    if filled_after is not None and u % 2 == 0:
                        last_unit = max(k for k, v in enumerate(UNIT_ORDER) if bank_of(v, False) == u // 2)
                        pe.wait_ge(E_ready, filled_after * E_UNITS + last_unit + 1)
                    cols = mlp_ps(b)[u // 2][:, (u % 2) * BATCH:(u % 2) * BATCH + n]
                    for c in range(PAIR_CHUNKS + 1):
                        rows = slice(0, PAIR_ROWS if c < PAIR_CHUNKS else 128)
                        for w, v in ((w1_hi, in_hi), (w1_hi, in_lo), (w1_lo, in_hi)):
                            inst = nc.tensor.matmul(cols, w[rows, c, u * 128:(u + 1) * 128], v[rows, c, 0:n],
                                                    start=(c == 0 and v is in_hi and w is w1_hi),
                                                    stop=(c == PAIR_CHUNKS and w is w1_lo))
                    if u % 2 == 1:
                        inst.then_inc(l1_done, 1)

            def keep_warm(bank, products):
                for _ in range(products):
                    nc.tensor.matmul(bank[:, 0:BATCH], w1_hi[:, PAIR_CHUNKS, 0:128], w1_hi[:, PAIR_CHUNKS, 0:BATCH],
                                     start=True, stop=True)

            def layer2(b, n):
                for u in range(H1 // 128):
                    if u % 2 == 0:
                        pe.wait_ge(h1_lo_ready, 2 * b + u // 2 + 1)
                    for m in range(H2 // 128):
                        for w, v in ((w2_hi, in_hi), (w2_hi, in_lo), (w2_lo, in_hi)):
                            inst = nc.tensor.matmul(mlp_ps(b)[2 + m][:, 0:n],
                                                    w[:, u, m * 128:(m + 1) * 128], v[:, u, 0:n],
                                                    start=(u == 0 and v is in_hi and w is w2_hi),
                                                    stop=(u == H1 // 128 - 1 and w is w2_lo))
                inst.then_inc(l2_done, 1)

            def layer3(b, n):
                pe.wait_ge(h2_ready, 2 * (b + 1))
                for t in range(n // TILE):
                    for m in range(H2 // 128):
                        inst = nc.tensor.matmul(mlp_ps(b)[1][:, t:t + 1], h2_sb[:, m, t * TILE:(t + 1) * TILE],
                                                w3_sb[:, m:m + 1], start=(m == 0), stop=(m == H2 // 128 - 1))
                inst.then_inc(l3_done, 1)

            def step(b, parity, visit, n):
                first, last = is_number(b, 0), is_number(b, LAST)
                if first:
                    first_fill()
                    pe.wait_ge(weights_loaded, 3 * 16)
                    pe.wait_ge(w1_lo_ready, 1)
                    pe.wait_ge(w2_lo_ready, 1)
                else:
                    fill(b, parity, visit, n)
                if not first and not last:
                    layer1(b - 1, before(b), filled_after=b)
                pe.wait_ge(E_ready, (b + 1) * E_UNITS)
                for w in range(GRAM_UNITS_OF[n]):
                    if not (first and w < GRAM_BANKS):
                        pe.wait_ge(gram_copied_dve if w % 2 else gram_copied_act,
                                   copied_before(b) + (w - GRAM_BANKS) // 2 + 1)
                    for gg in range(GRAM_GROUPS):
                        g = w * GRAM_GROUPS + gg
                        four = E[:, 4 * g:4 * g + 4, :]
                        inst = nc.tensor.matmul(
                            gram_ps[w % GRAM_BANKS][0:4 * FEATURES, gg * 4 * FEATURES:(gg + 1) * 4 * FEATURES],
                            four.rearrange("d s f -> d (s f)"), four.rearrange("d s f -> d (s f)"), start=True, stop=True)
                    inst.then_inc(gram_done, 1)
                    if not first and not last and w == LAYER2_AT:
                        layer2(b - 1, before(b))
                    if not first and not last and w == LAYER3_AT:
                        layer3(b - 1, before(b))
                if not first and not last:
                    pe.wait_ge(y_ready, b)

            pe.wait_ge(consts_ready, 1)
            batches(pe, step)
            keep_warm(fill_ps[3], WARM[0])
            layer1(LAST - 1, BATCH)
            keep_warm(fill_ps[3], WARM[1])
            layer2(LAST - 1, BATCH)
            keep_warm(fill_ps[0], WARM[2])
            layer1(LAST, HALF)
            layer3(LAST - 1, BATCH)
            keep_warm(fill_ps[0], WARM[3])
            layer2(LAST, HALF)
            layer3(LAST, HALF)
            pe.wait_ge(y_ready, BATCHES)
            nc.tensor.transpose(mlp_ps(LAST)[0][0:SAMPLES // TILE, 0:TILE], y_cols[:, :], ident[:, :])\
                .then_inc(y_transposed, 1)


def kernel(**inputs):
    import concourse.bacc as _bacc
    from concourse.bass_utils import run_bass_kernel_spmd as _run

    nc = _bacc.Bacc("TRN2", target_bir_lowering=False, num_devices=1)
    ids = np.asarray(inputs["ids"])
    x, w1 = np.asarray(inputs["r_dense_x"]), np.asarray(inputs["W_top1"])
    arrays = {
        "x": np.concatenate([x, np.zeros((HALF, D), x.dtype)]),
        "ids": np.ascontiguousarray(ids[:, GATHERED + LAST_EXTRA]),
        "ids_t": np.concatenate([ids[:, ONEHOT].T, np.zeros((NOH, HALF), ids.dtype)], axis=1),
    }
    for n, f in enumerate(ONEHOT + GATHERED):
        arrays[f"table_{n}"] = np.asarray(inputs[f"tbl_{f}"])
    arrays["w1_pairs"] = np.ascontiguousarray(w1[pair_rows()]).reshape(PAIR_CHUNKS, PAIR_ROWS, H1)
    arrays["w1_dense"] = np.ascontiguousarray(w1[PAIRS:])
    arrays["b1"] = np.ascontiguousarray(np.asarray(inputs["b_top1"]).reshape(-1, 128).T)
    arrays["w2"] = np.asarray(inputs["W_top2"])
    arrays["b2"] = np.ascontiguousarray(np.asarray(inputs["b_top2"]).reshape(-1, 128).T)
    arrays["w3"] = np.ascontiguousarray(np.asarray(inputs["W_top3"]).reshape(-1, 128).T)
    aps = {k: nc.dram_tensor(f"{k}_in", a.shape, mybir.dt.from_np(a.dtype), kind="ExternalInput").ap()
           for k, a in arrays.items()}
    y = nc.dram_tensor("y_out", (SAMPLES,), mybir.dt.float32, kind="ExternalOutput").ap()
    tables = [aps[f"table_{n}"] for n in range(TABLES)]
    dlrm_tower(nc, aps["x"], aps["ids"], aps["ids_t"], tables, aps["w1_pairs"], aps["w1_dense"],
               aps["b1"], aps["w2"], aps["b2"], aps["w3"], y)
    got = _run(nc, [{f"{k}_in": a for k, a in arrays.items()}], core_ids=[0])
    return got.results[0]["y_out"].reshape(SAMPLES, 1)
```

```python
import numpy as np
import concourse.bass as bass
from concourse import mybir
from contextlib import ExitStack

TABLES = 26
FEATURES = TABLES + 1
D = 128
SAMPLES = 2048
H1, H2 = 512, 256
SMALL_PARTS = 125

BATCH = 256
HALF = BATCH // 2
BATCHES = (SAMPLES - 2 * HALF) // BATCH + 2
LAST = BATCHES - 1
TILE = 128
TILES = BATCH // TILE
QUADS = BATCH // 4

TABLE_ROWS = [1000, 1250, 125000, 1250, 1250, 12500, 1000, 1250, 1250, 1250, 1250, 1000, 1250,
              1000, 1000, 1000, 1000, 1250, 12500, 12500, 1000, 12500, 12500, 1250, 1000, 1000]
ONEHOT_COUNT = 8
ONEHOT = sorted((f for f in range(TABLES) if TABLE_ROWS[f] <= 1250),
                key=lambda f: (TABLE_ROWS[f], f))[:ONEHOT_COUNT]
GATHERED = [f for f in range(TABLES) if f not in ONEHOT]
NOH, NG = len(ONEHOT), len(GATHERED)
ONEHOT_OF = {LAST - 1: NOH // 2, LAST: 0}
EXTRAS = {b: [(t, n) for t in range(tiles) for n in range(ONEHOT_OF[b], NOH)]
          for b, tiles in ((LAST - 1, TILES), (LAST, 1))}
EXTRA_SLOT = {(b, *extra): slot for slot, (b, extra) in
              enumerate((b, extra) for b in EXTRAS for extra in EXTRAS[b])}
EXTRA_TILES = TILES + 1


def onehot_of(b):
    return ONEHOT_OF.get(b, NOH) if isinstance(b, int) else NOH


FEATURE_AT = [f for pair in zip(ONEHOT, GATHERED) for f in pair] + GATHERED[NOH:] + [TABLES]
assert all(TABLE_ROWS[f] == 1000 for f in ONEHOT)
CHUNKS = TABLE_ROWS[ONEHOT[0]] // SMALL_PARTS

SHIFTS = (FEATURES - 1) // 2
PAIRS = FEATURES * SHIFTS
PAIR_CHUNKS = 3
PAIR_ROWS = PAIRS // PAIR_CHUNKS
WIDE = FEATURES + SHIFTS

E_UNITS = (FEATURES + 1) // 2
FILL_BANKS = 4


def unit_order():
    order, other = [], NOH
    for u in range(NOH):
        until = NOH + (E_UNITS - NOH) * (u + 1) // NOH
        order += [u, *range(other, until)]
        other = until
    return order


FIRST_ORDER = list(range(E_UNITS))
UNIT_ORDER = unit_order()

GRAM_GROUPS = 4
GRAM_UNITS_OF = {n: n // 4 // GRAM_GROUPS for n in (HALF, BATCH)}
GRAM_BANKS = 4
GRAM_STORES, PAIR_REORDERS = 2, 4

HALVES = 2
BLOCK_CHUNKS = CHUNKS // HALVES
OH_UNITS = NOH * HALVES
OH_SLOTS = 4
OH_AHEAD = 4
BLOCKS_AT = {HALF: (1, 3, 5, 7), BATCH: (3, 7, 9, 13)}
ID_UNITS = NOH // 2
RAW_IN_E = BATCH * FEATURES // (CHUNKS * D)

MLP_STEPS = {"tensor": {-1: "layer 1", 2: "layer 2", 5: "layer 3"},
             "scalar": {-1: "relu 1", 0: "relu 2", 6: "copy y"},
             "vector": {-1: "split, split h1"}}
INPUT_SPLIT_AT = 10
LATE_MLP_STEPS = {"tensor": {15: "layer 1"},
                  "scalar": {4: "split", 14: "relu 1"},
                  "vector": {5: "split", 15: "split h1"}}


def mlp_step(engine, b, w):
    if isinstance(b, int) and b in (0, LAST):
        return ""
    late = isinstance(b, int) and b == LAST - 1
    return (LATE_MLP_STEPS if late else MLP_STEPS)[engine].get(w, "")


def bank_of(u, first):
    if u < NOH:
        return u if first else u % 2
    return 2 + u % 2


def bank_freed_by(order, k, first):
    earlier = [j for j in range(k) if bank_of(order[j], first) == bank_of(order[k], first)]
    return earlier[-1] + 1 if earlier else 0


def pair_rows():
    number = {}
    for a in range(FEATURES):
        for b in range(a + 1, FEATURES):
            number[a, b] = len(number)
    rows = []
    for i in range(FEATURES):
        for k in range(1, SHIFTS + 1):
            a, b = FEATURE_AT[i], FEATURE_AT[(i + k) % FEATURES]
            rows.append(number[min(a, b), max(a, b)])
    return rows


def dlrm_tower(nc, x, ids, ids_t, tables, w1_pairs, w1_dense, b1, w2, b2, w3, y):
    fp32, fp32r, i32 = mybir.dt.float32, mybir.dt.float32r, mybir.dt.int32
    ALU, ACT = mybir.AluOpType, mybir.ActivationFunctionType

    ctx = ExitStack()
    with ctx:
        def sb(name, shape, dt=fp32):
            return ctx.enter_context(nc.sbuf_tensor(name, shape, dt))

        def pb(name):
            return ctx.enter_context(nc.psum_tensor(name, [128, 512], fp32))

        def sem(name):
            return ctx.enter_context(nc.semaphore(name))

        table_hi = sb("table_hi", [SMALL_PARTS, NOH * CHUNKS, D], fp32r)
        table_lo = sb("table_lo", [SMALL_PARTS, NOH * CHUNKS, D], fp32r)
        onehot = sb("onehot", [128, OH_SLOTS, BLOCK_CHUNKS, BATCH], fp32r)
        ids_row = sb("ids_row", [SMALL_PARTS, NOH, BATCH], i32)
        row_number = sb("row_number", [SMALL_PARTS, CHUNKS])
        row_int = sb("row_int", [SMALL_PARTS, CHUNKS], i32)
        all_ids = sb("all_ids", [TILE, SAMPLES // TILE, NG], i32)
        extra_ids = sb("extra_ids", [TILE, EXTRA_TILES, NOH], i32)
        gather_ids = sb("gather_ids", [TILE, 2, TILES, NG], i32)
        gathered = sb("gathered", [TILE, 2 * TILES, NG, D])
        dense_rows = sb("dense_rows", [TILE, 2, TILES, D])
        ident = sb("ident", [128, 128])
        E = sb("E", [D, BATCH, FEATURES])
        dense_t = sb("dense_t", [D, 2, BATCH])
        gram_sb = sb("gram_sb", [128, FEATURES * QUADS])
        pairs_t = sb("pairs_t", [PAIR_ROWS, PAIR_CHUNKS, BATCH])
        w1_hi = sb("w1_hi", [128, PAIR_CHUNKS + 1, H1], fp32r)
        w1_lo = sb("w1_lo", [128, PAIR_CHUNKS + 1, H1], fp32r)
        in_hi = sb("in_hi", [128, PAIR_CHUNKS + 1, BATCH], fp32r)
        in_lo = sb("in_lo", [128, PAIR_CHUNKS + 1, BATCH], fp32r)
        w2_hi = sb("w2_hi", [128, H1 // 128, H2], fp32r)
        w2_lo = sb("w2_lo", [128, H1 // 128, H2], fp32r)
        w3_sb = sb("w3_sb", [128, H2 // 128])
        b1_sb = sb("b1_sb", [128, H1 // 128])
        b2_sb = sb("b2_sb", [128, H2 // 128])
        h1_sb = sb("h1_sb", [128, H1 // 128, BATCH])
        h2_sb = sb("h2_sb", [128, H2 // 128, BATCH])
        y_cols = sb("y_cols", [TILE, SAMPLES // TILE])
        y_rows = sb("y_rows", [SAMPLES // TILE, TILE])
        in_E = [E[:, :, :].rearrange("p s f -> p (s f)")[:, n * CHUNKS * D:(n + 1) * CHUNKS * D]
                for n in range(RAW_IN_E)]
        raw_places = in_E + [gram_sb[:, n * CHUNKS * D:(n + 1) * CHUNKS * D]
                             for n in range(NOH - 1 - RAW_IN_E)]
        raw = [raw_places[n % len(raw_places)][0:SMALL_PARTS, :].rearrange("p (c d) -> p c d", d=D)
               for n in range(NOH)]
        raw_w1 = gathered[:, 1, 0:16, :].rearrange("p n d -> p (n d)").rearrange("p (c m) -> p c m", m=H1)
        raw_w2 = in_E[1].rearrange("p (c n) -> p c n", n=H2)
        table_part = [slice(n * CHUNKS, (n + 1) * CHUNKS) for n in range(NOH)]

        gram_dram = {n: nc.dram_tensor(f"gram_dram{n}", [4 * FEATURES, WIDE, n // 4], fp32, kind="Internal").ap()
                     for n in (HALF, BATCH)}
        pairs_dram = {n: nc.dram_tensor(f"pairs_dram{n}", [PAIRS, 4, n // 4], fp32, kind="Internal").ap()
                      for n in (HALF, BATCH)}

        fill_ps = [pb(f"fill_ps{n}") for n in range(FILL_BANKS)]
        gram_ps = [pb(f"gram_ps{n}") for n in range(GRAM_BANKS)]
        unit_ps = fill_ps + gram_ps

        def mlp_ps(b):
            if is_number(b, LAST):
                return gram_ps
            return gram_ps[0:2] + fill_ps[2:4] if is_number(b, LAST - 2) else fill_ps

        sp_waits = sem("sp_waits")
        pool_waits = sem("pool_waits")
        const_step = sem("const_step")
        consts_ready = sem("consts_ready")
        rows_ready = sem("rows_ready")
        weights_loaded = sem("weights_loaded")
        raw_loaded = [sem(f"raw_loaded{n}") for n in range(NOH)]
        w2_loaded = sem("w2_loaded")
        w2_hi_ready = sem("w2_hi_ready")
        w2_lo_ready = sem("w2_lo_ready")
        w1_loaded = sem("w1_loaded")
        w1_hi_ready = sem("w1_hi_ready")
        w1_lo_ready = sem("w1_lo_ready")
        in_hi_ready = sem("in_hi_ready")
        in_lo_ready = sem("in_lo_ready")
        hi_ready = sem("hi_ready")
        lo_ready = sem("lo_ready")
        first_ids_loaded = sem("first_ids_loaded")
        other_ids_loaded = sem("other_ids_loaded")
        batch_ids_ready = sem("batch_ids_ready")
        dense_loaded = [sem(f"dense_loaded{p}") for p in range(2)]
        ids_loaded = [sem(f"ids_loaded{m}") for m in range(ID_UNITS)]
        rows_gathered = [sem(f"rows_gathered{s}") for s in range(2 * TILES)]
        extra_gathered = {b: sem(f"extra_gathered{b}") for b in EXTRAS}
        onehot_ready = sem("onehot_ready")
        onehot_used = sem("onehot_used")
        filled = sem("filled")
        E_ready = sem("E_ready")
        gram_done = sem("gram_done")
        block_copied_act = sem("block_copied_act")
        block_copied_dve = sem("block_copied_dve")
        gram_copied_act = sem("gram_copied_act")
        gram_copied_dve = sem("gram_copied_dve")
        gram_stored = sem("gram_stored")
        pairs_reordered = sem("pairs_reordered")
        pairs_loaded = sem("pairs_loaded")
        l1_done = sem("l1_done")
        h1_ready = sem("h1_ready")
        h1_hi_ready = sem("h1_hi_ready")
        h1_lo_ready = sem("h1_lo_ready")
        l2_done = sem("l2_done")
        h2_ready = sem("h2_ready")
        l3_done = sem("l3_done")
        y_ready = sem("y_ready")
        y_transposed = sem("y_transposed")
        y_rows_ready = sem("y_rows_ready")
        y_stored = sem("y_stored")

        block = ctx.enter_context(nc.Block())

        def batches(eng, step):
            step(0, 0, 0, HALF)
            step(1, 1, 0, BATCH)
            with eng.Fori(0, (BATCHES - 5) // 2) as i:
                step(2 * i + 2, 0, i + 1, BATCH)
                step(2 * i + 3, 1, i + 1, BATCH)
            step(LAST - 2, 0, LAST // 2 - 1, BATCH)
            step(LAST - 1, 1, LAST // 2 - 1, BATCH)
            step(LAST, 0, LAST // 2, HALF)

        def parts(b):
            if is_number(b, LAST):
                return onehot[:, 0, :, :], onehot[:, 1, :, :]
            return in_hi[:, :, :], in_lo[:, :, :]

        def h2(b):
            if is_number(b, LAST):
                return gram_sb[:, 0:H2 // 128 * HALF].rearrange("p (m s) -> p m s", m=H2 // 128)
            return h2_sb[:, :, :]

        def split_products(b, w_hi, w_lo):
            hi, lo = parts(b)
            return [(w_hi, hi), (w_hi, lo), (w_lo, hi)]

        def first_sample(b):
            return 0 if is_number(b, 0) else b * BATCH - HALF

        def is_number(b, number):
            return isinstance(b, int) and b == number

        def before(b):
            return HALF if is_number(b, 1) else BATCH

        def gram_units_before(b):
            return 0 if is_number(b, 0) else b * GRAM_UNITS_OF[BATCH] - GRAM_UNITS_OF[HALF]

        def gathers_until(parity, t, visit):
            return (visit + (0 if parity == 0 and t == 1 else 1)) * NG * 16

        def gram_view(n):
            return gram_sb[:, 0:FEATURES * n // 4].rearrange("p (j g) -> p j g", j=FEATURES)

        def copy_gram(eng, copy, block_copied, b, w, n, meanwhile=None):
            unit = copied_before(b) + w // 2
            for q in (3, 2, 1, 0):
                if q < 3:
                    eng.wait_ge(block_copied, 3 * unit + 3 - q)
                rows = slice(0, (q + 1) * FEATURES)
                src = gram_ps[w % GRAM_BANKS][rows, 0:GRAM_GROUPS * 4 * FEATURES]\
                    .rearrange("i (g q j) -> i g q j", g=GRAM_GROUPS, q=4)[:, :, q, :]
                dst = gram_view(n)[rows, :, w * GRAM_GROUPS:(w + 1) * GRAM_GROUPS]
                inst = copy(dst, src.rearrange("i g j -> i j g"))
                if q > 0:
                    inst.then_inc(block_copied, 1)
                if meanwhile is not None and q > 0:
                    meanwhile(3 - q)
            return inst

        def copied_before(b):
            return 0 if is_number(b, 0) else b * (GRAM_UNITS_OF[BATCH] // 2) - GRAM_UNITS_OF[HALF] // 2

        LAST_USE_OF_EXTRA_PLACE = (LAST - 1) * E_UNITS

        w1_parts = [(slice(0, PAIR_ROWS), slice(0, PAIR_CHUNKS)), (slice(0, 128), slice(PAIR_CHUNKS, PAIR_CHUNKS + 1))]

        def input_parts(parity, n):
            return [(pairs_t[:, :, 0:n], *w1_parts[0]), (dense_t[:, parity:parity + 1, 0:n], *w1_parts[1])]

        @block.sync
        def _(sp):
            def load_dense(b, parity, tiles):
                src = x[bass.ds(first_sample(b), tiles * TILE), :].rearrange("(t p) d -> p t d", p=TILE)
                sp.dma_start(dense_rows[:, parity, 0:tiles, :], src).then_inc(dense_loaded[parity], 16)

            def load_ids(b, m, n):
                src = ids_t[2 * m:2 * m + 2, bass.ds(first_sample(b), n)].unsqueeze(0)
                sp.dma_start(ids_row[:, 2 * m:2 * m + 2, 0:n], src.to_broadcast([SMALL_PARTS, 2, n]))\
                  .then_inc(ids_loaded[m], 16)

            def load_table(n):
                sp.dma_start(raw[n], tables[n].rearrange("(p c) d -> p c d", c=CHUNKS))\
                  .then_inc(raw_loaded[n], 16)

            by_tile = ids.rearrange("(t p) n -> p t n", p=TILE)
            sp.dma_start(all_ids[:, 0:1, :], by_tile[:, 0:1, 0:NG]).then_inc(first_ids_loaded, 16)
            for n in range(NOH - 1):
                load_table(n)
                if n % 2 == 0:
                    load_ids(0, n // 2, HALF)
            sp.dma_start(raw_w1[0:PAIR_ROWS, 0:PAIR_CHUNKS, :], w1_pairs.rearrange("c p n -> p c n"))\
              .then_inc(w1_loaded, 16)
            sp.dma_start(raw_w1[:, PAIR_CHUNKS, :], w1_dense).then_inc(w1_loaded, 16)
            sp.dma_start(all_ids[:, 1:, :], by_tile[:, 1:, 0:NG]).then_inc(other_ids_loaded, 16)
            sp.dma_start(extra_ids[:, :, :], by_tile[:, SAMPLES // TILE - EXTRA_TILES:, NG:])\
              .then_inc(other_ids_loaded, 16)
            load_dense(0, 0, 1)
            load_dense(1, 1, TILES)
            sp.wait_ge(lo_ready, 1)
            load_table(NOH - 1)
            sp.wait_ge(lo_ready, 2)
            sp.dma_start(raw_w2, w2.rearrange("(c p) n -> p c n", p=128)).then_inc(w2_loaded, 16)
            for dst, src in ((w3_sb[:, :], w3), (b1_sb[:, :], b1), (b2_sb[:, :], b2)):
                sp.dma_start(dst, src).then_inc(weights_loaded, 16)

            def wait_for(semaphore, value):
                sp.wait_ge(semaphore, value)
                sp.sem_inc(sp_waits, 1)

            def step(b, parity, visit, n):
                first, last = is_number(b, 0), is_number(b, LAST)
                quads = n // 4
                if not first and not last:
                    wait_for(filled, b * E_UNITS)
                    load_dense(b + 1, 1 - parity, 1 if is_number(b, LAST - 1) else TILES)
                if not last:
                    for m in range(onehot_of(b + 1) // 2):
                        wait_for(onehot_ready, b * OH_UNITS + 4 * (m + 1))
                        load_ids(b + 1, m, BATCH)
                if not first and not last:
                    wait_for(pairs_loaded, b * 16)
                wait_for(gram_copied_act, copied_before(b) + GRAM_UNITS_OF[n] // 2)
                wait_for(gram_copied_dve, copied_before(b) + GRAM_UNITS_OF[n] // 2)
                sp.dma_start(gram_dram[n][:, 0:FEATURES, :], gram_view(n)[0:4 * FEATURES, :, :])\
                  .then_inc(gram_stored, 16)
                sp.dma_start(gram_dram[n][:, FEATURES:WIDE, :], gram_view(n)[0:4 * FEATURES, 0:SHIFTS, :])\
                  .then_inc(gram_stored, 16)
                wait_for(gram_stored, (b + 1) * GRAM_STORES * 16)
                for q in range(4):
                    src = bass.AP(gram_dram[n].tensor, (FEATURES * q * WIDE + 1) * quads,
                                  [[(WIDE + 1) * quads, FEATURES], [quads, SHIFTS], [1, quads]])
                    sp.dma_start(pairs_dram[n][:, q, :].rearrange("(i k) g -> i k g", k=SHIFTS), src)\
                      .then_inc(pairs_reordered, 16)
                wait_for(pairs_reordered, (b + 1) * PAIR_REORDERS * 16)
                if last:
                    sp.wait_ge(in_lo_ready, LAST)
                sp.dma_start(pairs_t[:, :, 0:n], pairs_dram[n].rearrange("(c r) q g -> r c (q g)", c=PAIR_CHUNKS))\
                  .then_inc(pairs_loaded, 16)

            batches(sp, step)
            sp.wait_ge(y_rows_ready, 1)
            sp.dma_start(y.rearrange("(t p) -> t p", p=TILE), y_rows[:, :]).then_inc(y_stored, 16)
            sp.wait_ge(y_stored, 16)

        @block.gpsimd
        def _(pool):
            pool.iota(row_int[:, :], pattern=[[1, CHUNKS]], base=0, channel_multiplier=CHUNKS)\
                .then_inc(const_step, 1)
            pool.memset(ident[:, :], 0.0).then_inc(const_step, 1)
            pool.wait_ge(const_step, 2)
            pool.tensor_copy(row_number[:, :], row_int[:, :]).then_inc(rows_ready, 1)
            pool.affine_select(out=ident[:, :], in_=ident[:, :], compare_op=ALU.not_equal, fill=1.0,
                               base=0, pattern=[[-1, 128]], channel_multiplier=1).then_inc(consts_ready, 1)

            def step(b, parity, visit, n):
                tiles = n // TILE
                if is_number(b, 0):
                    pool.wait_ge(first_ids_loaded, 16)
                    ids_of_batch = all_ids[:, 0:1, :]
                else:
                    pool.wait_ge(other_ids_loaded, 2 * 16)
                    if not is_number(b, 1):
                        pool.wait_ge(filled, (b - 1) * E_UNITS)
                        pool.wait_ge(w1_lo_ready, 1)
                    ids_of_batch = all_ids[:, bass.ds(b * TILES - 1, tiles), :]
                pool.tensor_copy(gather_ids[:, parity, 0:tiles, :], ids_of_batch).then_inc(batch_ids_ready, 1)
                pool.wait_ge(batch_ids_ready, b + 1)
                pool.sem_inc(pool_waits, 1)
                for t in range(tiles):
                    for g in range(NG):
                        pool.indirect_dma_start(
                            out=gathered[:, parity * TILES + t, g, :], out_offset=None,
                            in_=tables[NOH + g],
                            in_offset=bass.IndirectOffsetOnAxis(ap=gather_ids[:, parity, t, g:g + 1], axis=0),
                        ).then_inc(rows_gathered[parity * TILES + t], 16)
                if isinstance(b, int) and b in EXTRAS:
                    pool.wait_ge(filled, LAST_USE_OF_EXTRA_PLACE)
                    for t, g in EXTRAS[b]:
                        pool.indirect_dma_start(
                            out=gathered[:, 1, EXTRA_SLOT[b, t, g], :], out_offset=None, in_=tables[g],
                            in_offset=bass.IndirectOffsetOnAxis(
                                ap=extra_ids[:, (b - LAST + 1) * TILES + t, g:g + 1], axis=0),
                        ).then_inc(extra_gathered[b], 16)

            batches(pool, step)

        @block.scalar
        def _(act):
            def take_hi(n):
                act.wait_ge(raw_loaded[n], 16)
                nc.scalar.activation(table_hi[:, table_part[n], :], raw[n], ACT.Copy).then_inc(hi_ready, 1)

            def take_input_hi(b, parity, n):
                if not is_number(b, 0) and not is_number(b, LAST):
                    act.wait_ge(l2_done, b)
                act.wait_ge(pairs_loaded, 16 * (b + 1))
                for src, rows, chunks in input_parts(parity, n):
                    inst = nc.scalar.activation(parts(b)[0][rows, chunks, 0:n], src, ACT.Copy)
                inst.then_inc(in_hi_ready, 1)

            def relu1(b, n):
                def relu(half):
                    for u in (2 * half, 2 * half + 1):
                        columns = mlp_ps(b)[half][:, (u % 2) * BATCH:(u % 2) * BATCH + n]
                        nc.scalar.activation(h1_sb[:, u, 0:n], columns, ACT.Relu,
                                             bias=b1_sb[:, u:u + 1]).then_inc(h1_ready, 1)

                def take_hi(half):
                    part = slice(2 * half, 2 * half + 2)
                    act.wait_ge(h1_ready, 4 * b + 2 * half + 2)
                    nc.scalar.activation(parts(b)[0][:, part, 0:n], h1_sb[:, part, 0:n], ACT.Copy)\
                        .then_inc(h1_hi_ready, 1)

                act.wait_ge(l1_done, 2 * b + 1)
                relu(0)
                act.wait_ge(l1_done, 2 * b + 2)
                take_hi(0)
                relu(1)
                take_hi(1)

            def relu2(b, n):
                act.wait_ge(l2_done, b + 1)
                for m in range(H2 // 128):
                    nc.scalar.activation(h2(b)[:, m, 0:n].rearrange("p (g q) -> p q g", q=4),
                                         mlp_ps(b)[2 + m][:, 0:n].rearrange("p (q g) -> p q g", q=4),
                                         ACT.Relu, bias=b2_sb[:, m:m + 1]).then_inc(h2_ready, 1)

            def copy_y(b, n):
                act.wait_ge(l3_done, b + 1)
                tile = 0 if is_number(b, 0) else b * TILES - 1
                nc.scalar.activation(y_cols[:, bass.ds(tile, n // TILE)], mlp_ps(b)[1][:, 0:n // TILE],
                                     ACT.Copy).then_inc(y_ready, 1)

            def run_mlp(b, parity, w):
                todo = mlp_step("scalar", b, w)
                if todo == "split":
                    take_input_hi(b - 1, 1 - parity, before(b))
                elif todo == "relu 1":
                    relu1(b - 1, before(b))
                elif todo == "relu 2":
                    relu2(b - 1, before(b))
                elif todo == "copy y":
                    copy_y(b - 1, before(b))

            def step(b, parity, visit, n):
                first, last = is_number(b, 0), is_number(b, LAST)
                for k, u in enumerate(FIRST_ORDER if first else UNIT_ORDER):
                    if k == INPUT_SPLIT_AT and mlp_step("scalar", b, -1):
                        take_input_hi(b - 1, 1 - parity, before(b))
                    act.wait_ge(filled, b * E_UNITS + k + 1)
                    src = unit_ps[bank_of(u, first)]
                    if u < E_UNITS - 1:
                        nc.scalar.activation(E[:, 0:n, 2 * u:2 * u + 2].rearrange("d s f -> d f s"),
                                             src[:, :].rearrange("d (f s) -> d f s", f=2)[:, :, 0:n],
                                             ACT.Copy).then_inc(E_ready, 1)
                    else:
                        nc.scalar.activation(E[:, 0:n, FEATURES - 1], src[:, 0:n], ACT.Copy)
                        nc.scalar.activation(dense_t[:, parity, 0:n].rearrange("d (q g) -> d q g", q=4),
                                             src[:, 0:n].rearrange("d (g q) -> d q g", q=4),
                                             ACT.Copy).then_inc(E_ready, 1)
                if first:
                    act.wait_ge(weights_loaded, 3 * 16)
                run_mlp(b, parity, -1)
                for w in range(0, GRAM_UNITS_OF[n], 2):
                    act.wait_ge(gram_done, gram_units_before(b) + w + 1)
                    if w == 0 and not first:
                        act.wait_ge(gram_stored, b * GRAM_STORES * 16)
                    copy_gram(act, nc.scalar.copy, block_copied_act, b, w, n).then_inc(gram_copied_act, 1)
                    run_mlp(b, parity, w)

            for n in range(NOH):
                take_hi(n)
            act.wait_ge(w1_loaded, 2 * 16)
            for rows, chunks in w1_parts:
                inst = nc.scalar.activation(w1_hi[rows, chunks, :], raw_w1[rows, chunks, :], ACT.Copy)
            inst.then_inc(w1_hi_ready, 1)
            act.wait_ge(w2_loaded, 16)
            nc.scalar.activation(w2_hi[:, :, :], raw_w2, ACT.Copy).then_inc(w2_hi_ready, 1)
            act.wait_ge(lo_ready, NOH)
            act.wait_ge(w2_lo_ready, 1)
            batches(act, step)
            relu2(LAST - 2, BATCH)
            take_input_hi(LAST - 1, 1, BATCH)
            copy_y(LAST - 2, BATCH)
            relu1(LAST - 1, BATCH)
            take_input_hi(LAST, 0, HALF)
            relu2(LAST - 1, BATCH)
            relu1(LAST, HALF)
            relu2(LAST, HALF)
            copy_y(LAST - 1, BATCH)
            copy_y(LAST, HALF)
            act.wait_ge(y_transposed, 1)
            nc.scalar.activation(y_rows[:, :], mlp_ps(LAST)[0][0:SAMPLES // TILE, 0:TILE], ACT.Copy)\
                .then_inc(y_rows_ready, 1)

        @block.vector
        def _(dve):
            def take_lo(n):
                dve.wait_ge(hi_ready, n + 1)
                part = table_part[n]
                nc.vector.tensor_tensor(table_lo[:, part, :], raw[n], table_hi[:, part, :].bitcast(fp32),
                                        ALU.subtract).then_inc(lo_ready, 1)

            def split_weights():
                dve.wait_ge(w1_hi_ready, 1)
                for rows, chunks in w1_parts:
                    inst = nc.vector.tensor_tensor(w1_lo[rows, chunks, :], raw_w1[rows, chunks, :],
                                                   w1_hi[rows, chunks, :].bitcast(fp32), ALU.subtract)
                inst.then_inc(w1_lo_ready, 1)
                dve.wait_ge(w2_hi_ready, 1)
                nc.vector.tensor_tensor(w2_lo[:, :, :], raw_w2, w2_hi[:, :, :].bitcast(fp32), ALU.subtract)\
                    .then_inc(w2_lo_ready, 1)

            def take_input_lo(b, parity, n):
                dve.wait_ge(in_hi_ready, b + 1)
                for src, rows, chunks in input_parts(parity, n):
                    inst = nc.vector.tensor_tensor(parts(b)[1][rows, chunks, 0:n], src,
                                                   parts(b)[0][rows, chunks, 0:n].bitcast(fp32), ALU.subtract)
                inst.then_inc(in_lo_ready, 1)

            def take_h1_lo(b, n):
                for half in range(2):
                    part = slice(2 * half, 2 * half + 2)
                    dve.wait_ge(h1_hi_ready, 2 * b + half + 1)
                    nc.vector.tensor_tensor(parts(b)[1][:, part, 0:n], h1_sb[:, part, 0:n],
                                            parts(b)[0][:, part, 0:n].bitcast(fp32), ALU.subtract)\
                        .then_inc(h1_lo_ready, 1)

            def onehot_chunk(b, u, c, n):
                table, h = u // HALVES, u % HALVES
                if c == 0:
                    if u % (2 * HALVES) == 0:
                        dve.wait_ge(ids_loaded[table // 2], 16 * (b + 1))
                    if not (is_number(b, 0) and u < OH_SLOTS):
                        dve.wait_ge(onehot_used, b * OH_UNITS + u - OH_SLOTS + 1)
                col = h * BLOCK_CHUNKS + c
                inst = nc.vector.tensor_scalar(onehot[0:SMALL_PARTS, u % OH_SLOTS, c, 0:n], ids_row[:, table, 0:n],
                                               row_number[:, col:col + 1], None, ALU.is_equal)
                if c == BLOCK_CHUNKS - 1:
                    inst.then_inc(onehot_ready, 1)

            def make_onehot(b, u, n):
                for c in range(BLOCK_CHUNKS):
                    onehot_chunk(b, u, c, n)

            def run_mlp(b, parity, w):
                todo = mlp_step("vector", b, w)
                if "split" in todo.split(", "):
                    take_input_lo(b - 1, 1 - parity, before(b))
                if "split h1" in todo:
                    take_h1_lo(b - 1, before(b))

            def step(b, parity, visit, n):
                first, last = is_number(b, 0), is_number(b, LAST)
                if not last:
                    for u in range(OH_AHEAD, onehot_of(b) * HALVES):
                        make_onehot(b, u, n)
                        if first and u == OH_AHEAD + OH_SLOTS - 1:
                            split_weights()
                run_mlp(b, parity, -1)
                for w in range(1, GRAM_UNITS_OF[n], 2):
                    dve.wait_ge(gram_done, gram_units_before(b) + w + 1)
                    if w == 1 and not first:
                        dve.wait_ge(gram_stored, b * GRAM_STORES * 16)
                    ahead = not last and onehot_of(b + 1) > 0 and w in BLOCKS_AT[n]
                    block = BLOCKS_AT[n].index(w) if ahead else None
                    between = (lambda c: onehot_chunk(b + 1, block, c, BATCH)) if ahead else None
                    copy_gram(dve, nc.vector.tensor_copy, block_copied_dve, b, w, n, between)\
                        .then_inc(gram_copied_dve, 1)
                    if ahead:
                        onehot_chunk(b + 1, block, BLOCK_CHUNKS - 1, BATCH)
                    run_mlp(b, parity, w)

            dve.wait_ge(rows_ready, 1)
            for n in range(NOH):
                take_lo(n)
                for u in range(n * HALVES, min((n + 1) * HALVES, OH_AHEAD)):
                    make_onehot(0, u, HALF)
            batches(dve, step)
            take_input_lo(LAST - 1, 1, BATCH)
            take_h1_lo(LAST - 1, BATCH)
            take_input_lo(LAST, 0, HALF)
            take_h1_lo(LAST, HALF)

        @block.tensor
        def _(pe):
            def lookup(b, table, cols, n):
                if is_number(b, 0):
                    pe.wait_ge(lo_ready, table + 1)
                for h in range(HALVES):
                    block_number = table * HALVES + h
                    pe.wait_ge(onehot_ready, b * OH_UNITS + block_number + 1)
                    for c in range(BLOCK_CHUNKS):
                        for part in (table_hi, table_lo):
                            inst = nc.tensor.matmul(
                                cols, part[:, table * CHUNKS + h * BLOCK_CHUNKS + c, :],
                                onehot[0:SMALL_PARTS, block_number % OH_SLOTS, c, 0:n],
                                start=(h == 0 and c == 0 and part is table_hi),
                                stop=(h == 1 and c == BLOCK_CHUNKS - 1 and part is table_lo))
                    inst.then_inc(onehot_used, 1)
                return inst

            def columns(u, pos, first, n):
                at = (pos % 2) * BATCH
                return unit_ps[bank_of(u, first)][:, at:at + n]

            def transposed(cols, b, parity, pos, tiles):
                g = pos // 2 if pos < 2 * NOH else pos - NOH
                for t in range(tiles):
                    if pos == FEATURES - 1:
                        rows = dense_rows[:, parity, t, :]
                    elif pos < 2 * NOH and pos % 2 == 0:
                        rows = gathered[:, 1, EXTRA_SLOT[b, t, pos // 2], :]
                    else:
                        rows = gathered[:, parity * TILES + t, g, :]
                    inst = nc.tensor.transpose(cols[:, t * TILE:(t + 1) * TILE], rows, ident[:, :])
                return inst

            def first_fill():
                for u in range(NOH):
                    lookup(0, u, columns(u, 2 * u, True, HALF), HALF)
                pe.wait_ge(rows_gathered[0], gathers_until(0, 0, 0))
                for u in range(NOH):
                    transposed(columns(u, 2 * u + 1, True, HALF), 0, 0, 2 * u + 1, 1).then_inc(filled, 1)
                pe.wait_ge(dense_loaded[0], 16)
                for u in range(NOH, E_UNITS):
                    pe.wait_ge(E_ready, bank_freed_by(FIRST_ORDER, u, True))
                    for pos in range(2 * u, min(2 * u + 2, FEATURES)):
                        inst = transposed(columns(u, pos, True, HALF), 0, 0, pos, 1)
                    inst.then_inc(filled, 1)

            def fill(b, parity, visit, n):
                tiles = n // TILE
                for k, u in enumerate(UNIT_ORDER):
                    freed = bank_freed_by(UNIT_ORDER, k, False)
                    if freed:
                        pe.wait_ge(E_ready, b * E_UNITS + freed)
                    by_lookup = u < onehot_of(b)
                    if k == 0 and is_number(b, 1):
                        for early in UNIT_ORDER[0:2]:
                            lookup(b, early, columns(early, 2 * early, False, n), n)
                    elif by_lookup and not (k == 1 and is_number(b, 1)):
                        lookup(b, u, columns(u, 2 * u, False, n), n)
                    if k == 0:
                        for t in range(tiles):
                            pe.wait_ge(rows_gathered[parity * TILES + t], gathers_until(parity, t, visit))
                    if u == onehot_of(b) and u < NOH:
                        pe.wait_ge(extra_gathered[b], 16 * len(EXTRAS[b]))
                    for pos in range(2 * u, min(2 * u + 2, FEATURES)):
                        if pos == FEATURES - 1:
                            pe.wait_ge(dense_loaded[parity], (visit + 1) * 16)
                        if not by_lookup or pos % 2 == 1:
                            inst = transposed(columns(u, pos, False, n), b, parity, pos, tiles)
                    inst.then_inc(filled, 1)

            def layer1(b, n, filled_after=None):
                pe.wait_ge(in_lo_ready, b + 1)
                for u in range(H1 // 128):
                    if filled_after is not None and u % 2 == 0:
                        last_unit = max(k for k, v in enumerate(UNIT_ORDER) if bank_of(v, False) == u // 2)
                        pe.wait_ge(E_ready, filled_after * E_UNITS + last_unit + 1)
                    cols = mlp_ps(b)[u // 2][:, (u % 2) * BATCH:(u % 2) * BATCH + n]
                    for c in range(PAIR_CHUNKS + 1):
                        rows = slice(0, PAIR_ROWS if c < PAIR_CHUNKS else 128)
                        for p, (w, v) in enumerate(split_products(b, w1_hi, w1_lo)):
                            inst = nc.tensor.matmul(cols, w[rows, c, u * 128:(u + 1) * 128], v[rows, c, 0:n],
                                                    start=(c == 0 and p == 0), stop=(c == PAIR_CHUNKS and p == 2))
                    if u % 2 == 1:
                        inst.then_inc(l1_done, 1)

            def keep_warm(bank, products):
                for _ in range(products):
                    nc.tensor.matmul(bank[:, 0:BATCH], w1_hi[:, PAIR_CHUNKS, 0:128], w1_hi[:, PAIR_CHUNKS, 0:BATCH],
                                     start=True, stop=True)

            def layer2(b, n):
                for u in range(H1 // 128):
                    if u % 2 == 0:
                        pe.wait_ge(h1_lo_ready, 2 * b + u // 2 + 1)
                    for m in range(H2 // 128):
                        for p, (w, v) in enumerate(split_products(b, w2_hi, w2_lo)):
                            inst = nc.tensor.matmul(mlp_ps(b)[2 + m][:, 0:n],
                                                    w[:, u, m * 128:(m + 1) * 128], v[:, u, 0:n],
                                                    start=(u == 0 and p == 0),
                                                    stop=(u == H1 // 128 - 1 and p == 2))
                inst.then_inc(l2_done, 1)

            def layer3(b, n):
                pe.wait_ge(h2_ready, 2 * (b + 1))
                for t in range(n // TILE):
                    for m in range(H2 // 128):
                        inst = nc.tensor.matmul(mlp_ps(b)[1][:, t:t + 1], h2(b)[:, m, t * TILE:(t + 1) * TILE],
                                                w3_sb[:, m:m + 1], start=(m == 0), stop=(m == H2 // 128 - 1))
                inst.then_inc(l3_done, 1)

            def run_mlp(b, w):
                todo = mlp_step("tensor", b, w)
                if todo == "layer 1":
                    if is_number(b, LAST - 1):
                        pe.wait_ge(gram_copied_act, copied_before(b) + GRAM_UNITS_OF[BATCH] // 2 - 1)
                        pe.wait_ge(gram_copied_dve, copied_before(b) + GRAM_UNITS_OF[BATCH] // 2 - 1)
                    layer1(b - 1, before(b), filled_after=b)
                elif todo == "layer 2":
                    layer2(b - 1, before(b))
                elif todo == "layer 3":
                    layer3(b - 1, before(b))

            def step(b, parity, visit, n):
                first, last = is_number(b, 0), is_number(b, LAST)
                if first:
                    first_fill()
                    pe.wait_ge(weights_loaded, 3 * 16)
                    pe.wait_ge(w1_lo_ready, 1)
                    pe.wait_ge(w2_lo_ready, 1)
                else:
                    fill(b, parity, visit, n)
                run_mlp(b, -1)
                pe.wait_ge(E_ready, (b + 1) * E_UNITS)
                if last:
                    pe.wait_ge(h1_lo_ready, 2 * (LAST - 1))
                for w in range(GRAM_UNITS_OF[n]):
                    if not (first and w < GRAM_BANKS):
                        pe.wait_ge(gram_copied_dve if w % 2 else gram_copied_act,
                                   copied_before(b) + (w - GRAM_BANKS) // 2 + 1)
                    for gg in range(GRAM_GROUPS):
                        g = w * GRAM_GROUPS + gg
                        four = E[:, 4 * g:4 * g + 4, :].rearrange("d s f -> d (s f)")
                        inst = nc.tensor.matmul(
                            gram_ps[w % GRAM_BANKS][0:4 * FEATURES, gg * 4 * FEATURES:(gg + 1) * 4 * FEATURES],
                            four, four, start=True, stop=True)
                    inst.then_inc(gram_done, 1)
                    run_mlp(b, w)
                if not first and not last and not is_number(b, LAST - 1):
                    pe.wait_ge(y_ready, b)

            pe.wait_ge(consts_ready, 1)
            batches(pe, step)
            layer2(LAST - 2, BATCH)
            keep_warm(fill_ps[0], 10)
            pe.wait_ge(gram_copied_dve, copied_before(LAST) + GRAM_UNITS_OF[HALF] // 2)
            layer3(LAST - 2, BATCH)
            keep_warm(fill_ps[0], 13)
            layer1(LAST - 1, BATCH)
            keep_warm(fill_ps[3], 14)
            layer2(LAST - 1, BATCH)
            pe.wait_ge(y_ready, LAST - 1)
            layer1(LAST, HALF)
            keep_warm(fill_ps[0], 14)
            layer2(LAST, HALF)
            layer3(LAST - 1, BATCH)
            layer3(LAST, HALF)
            pe.wait_ge(y_ready, BATCHES)
            nc.tensor.transpose(mlp_ps(LAST)[0][0:SAMPLES // TILE, 0:TILE], y_cols[:, :], ident[:, :])\
                .then_inc(y_transposed, 1)


def kernel(**inputs):
    import concourse.bacc as _bacc
    from concourse.bass_utils import run_bass_kernel_spmd as _run

    nc = _bacc.Bacc("TRN2", target_bir_lowering=False, num_devices=1)
    ids = np.asarray(inputs["ids"])
    x, w1 = np.asarray(inputs["r_dense_x"]), np.asarray(inputs["W_top1"])
    arrays = {
        "x": x,
        "ids": np.ascontiguousarray(ids[:, GATHERED + ONEHOT]),
        "ids_t": np.ascontiguousarray(ids[:, ONEHOT].T),
    }
    for n, f in enumerate(ONEHOT + GATHERED):
        arrays[f"table_{n}"] = np.asarray(inputs[f"tbl_{f}"])
    arrays["w1_pairs"] = np.ascontiguousarray(w1[pair_rows()]).reshape(PAIR_CHUNKS, PAIR_ROWS, H1)
    arrays["w1_dense"] = np.ascontiguousarray(w1[PAIRS:])
    arrays["b1"] = np.ascontiguousarray(np.asarray(inputs["b_top1"]).reshape(-1, 128).T)
    arrays["w2"] = np.asarray(inputs["W_top2"])
    arrays["b2"] = np.ascontiguousarray(np.asarray(inputs["b_top2"]).reshape(-1, 128).T)
    arrays["w3"] = np.ascontiguousarray(np.asarray(inputs["W_top3"]).reshape(-1, 128).T)
    aps = {k: nc.dram_tensor(f"{k}_in", a.shape, mybir.dt.from_np(a.dtype), kind="ExternalInput").ap()
           for k, a in arrays.items()}
    y = nc.dram_tensor("y_out", (SAMPLES,), mybir.dt.float32, kind="ExternalOutput").ap()
    tables = [aps[f"table_{n}"] for n in range(TABLES)]
    dlrm_tower(nc, aps["x"], aps["ids"], aps["ids_t"], tables, aps["w1_pairs"], aps["w1_dense"],
               aps["b1"], aps["w2"], aps["b2"], aps["w3"], y)
    got = _run(nc, [{f"{k}_in": a for k, a in arrays.items()}], core_ids=[0])
    return got.results[0]["y_out"].reshape(SAMPLES, 1)
```
